# Optimizing a Trainium2 kernel written in Bass

```python
import numpy as np
import jax
import jax.numpy as jnp

def _softmax(x, axis=-1):
    return jax.nn.softmax(x, axis=axis)

def _gelu(x):
    return jax.nn.gelu(x, approximate=True)

def _silu(x):
    return jax.nn.silu(x)

def _sigmoid(x):
    return jax.nn.sigmoid(x)

def _layernorm(x, axis=-1, eps=1e-05):
    m = jnp.mean(x, axis=axis, keepdims=True)
    v = jnp.var(x, axis=axis, keepdims=True)
    return (x - m) / jnp.sqrt(v + eps)

def _scatter_add(tgt, idx, src, axis=0):
    return tgt.at[idx].add(src)

def _segment_sum(src, seg, n):
    return jax.ops.segment_sum(src, seg, n)
kernel_name = 'mk_recurrent_d1_jaxref_r8_16237b'

def setup_inputs(seed: int=0):
    np.random.seed(seed)
    _w = jnp.asarray

    def _L0_attn_setup():
        import jax, jax.numpy as jnp
        import numpy as np
        N_HEAD = 16
        N_EMBED = 256
        N_BLOCK = 256
        THETA = 10000.0

        def _rope_cos_sin(n_head, head_dim):
            freqs = THETA ** (-(jnp.arange(0, head_dim, 2, dtype=jnp.float32) / head_dim))
            t = jnp.arange(n_head, dtype=jnp.float32)
            ang = jnp.outer(t, freqs)
            return (jnp.cos(ang)[None, :, None, :], jnp.sin(ang)[None, :, None, :])

        def _apply_rope(x, cos, sin):
            B, H, T, hd = x.shape
            xp = x.reshape(B, H, T, hd // 2, 2)
            a, b = (xp[..., 0], xp[..., 1])
            out = jnp.stack([a * cos - b * sin, a * sin + b * cos], axis=-1)
            return out.reshape(B, H, T, hd)
        key = jax.random.key(seed)
        ks = jax.random.split(key, 5)
        E = N_EMBED
        x = jax.random.normal(ks[0], (2, 256, E), dtype=jnp.float32)
        s = 1.0 / np.sqrt(E)
        w_attn = jax.random.normal(ks[1], (E, 3 * E), dtype=jnp.float32) * s
        b_attn = jnp.zeros((3 * E,), dtype=jnp.float32)
        w_proj = jax.random.normal(ks[2], (E, E), dtype=jnp.float32) * s
        b_proj = jnp.zeros((E,), dtype=jnp.float32)
        return {'x': x, 'w_attn': w_attn, 'b_attn': b_attn, 'w_proj': w_proj, 'b_proj': b_proj}
    _L0_attn_in = _L0_attn_setup()

    def _L0_ffn_setup():
        import jax, jax.numpy as jnp
        import numpy as np
        ZERO_POINT = 128.0

        def _dequant(wq, scale):
            return (wq.astype(jnp.float32) - ZERO_POINT) * scale[:, None]
        key = jax.random.key(seed)
        ks = jax.random.split(key, 7)
        H, I = (256, 1024)
        B, S = (2, 256)
        hidden_state = jax.random.normal(ks[0], (B, S, H), dtype=jnp.float32)
        gate_w = jax.random.randint(ks[1], (I, H), 0, 32, dtype=jnp.int32)
        up_w = jax.random.randint(ks[2], (I, H), 0, 32, dtype=jnp.int32)
        down_w = jax.random.randint(ks[3], (H, I), 0, 32, dtype=jnp.int32)
        gate_scale = jax.random.uniform(ks[4], (I,), dtype=jnp.float32) * 0.02
        up_scale = jax.random.uniform(ks[5], (I,), dtype=jnp.float32) * 0.02
        down_scale = jax.random.uniform(ks[6], (H,), dtype=jnp.float32) * 0.02
        return {'hidden_state': hidden_state, 'gate_w': gate_w, 'gate_scale': gate_scale, 'up_w': up_w, 'up_scale': up_scale, 'down_w': down_w, 'down_scale': down_scale}
    _L0_ffn_in = _L0_ffn_setup()
    _d = {'L0_attn_x': _L0_attn_in['x'], 'L0_attn_w_attn': _L0_attn_in['w_attn'], 'L0_attn_b_attn': _L0_attn_in['b_attn'], 'L0_attn_w_proj': _L0_attn_in['w_proj'], 'L0_attn_b_proj': _L0_attn_in['b_proj'], 'L0_ffn_gate_w': _L0_ffn_in['gate_w'], 'L0_ffn_gate_scale': _L0_ffn_in['gate_scale'], 'L0_ffn_up_w': _L0_ffn_in['up_w'], 'L0_ffn_up_scale': _L0_ffn_in['up_scale'], 'L0_ffn_down_w': _L0_ffn_in['down_w'], 'L0_ffn_down_scale': _L0_ffn_in['down_scale']}
    _x0 = _d['L0_attn_x']
    _d['L0_attn_x'] = jax.random.normal(jax.random.fold_in(jax.random.key(seed), 1), (4, 1024, 256), dtype=_x0.dtype)
    del _x0
    return _d

def reference(L0_attn_x, L0_attn_w_attn, L0_attn_b_attn, L0_attn_w_proj, L0_attn_b_proj, L0_ffn_gate_w, L0_ffn_gate_scale, L0_ffn_up_w, L0_ffn_up_scale, L0_ffn_down_w, L0_ffn_down_scale):

    def _L0_attn_ref(x, w_attn, b_attn, w_proj, b_proj):
        import jax, jax.numpy as jnp
        import numpy as np
        N_HEAD = 16
        N_EMBED = 256
        N_BLOCK = 256
        THETA = 10000.0

        def _rope_cos_sin(n_head, head_dim):
            freqs = THETA ** (-(jnp.arange(0, head_dim, 2, dtype=jnp.float32) / head_dim))
            t = jnp.arange(n_head, dtype=jnp.float32)
            ang = jnp.outer(t, freqs)
            return (jnp.cos(ang)[None, :, None, :], jnp.sin(ang)[None, :, None, :])

        def _apply_rope(x, cos, sin):
            B, H, T, hd = x.shape
            xp = x.reshape(B, H, T, hd // 2, 2)
            a, b = (xp[..., 0], xp[..., 1])
            out = jnp.stack([a * cos - b * sin, a * sin + b * cos], axis=-1)
            return out.reshape(B, H, T, hd)
        B, T, E = x.shape
        H = N_HEAD
        hd = E // H
        qkv = x @ w_attn + b_attn
        q, k, v = jnp.split(qkv, 3, axis=-1)
        q = q.reshape(B, T, H, hd).transpose(0, 2, 1, 3)
        k = k.reshape(B, T, H, hd).transpose(0, 2, 1, 3)
        v = v.reshape(B, T, H, hd).transpose(0, 2, 1, 3)
        cos, sin = _rope_cos_sin(H, hd)
        q = _apply_rope(q, cos, sin)
        k = _apply_rope(k, cos, sin)
        scores = jnp.einsum('bhtd,bhsd->bhts', q, k)
        causal = jnp.tril(jnp.ones((T, T), dtype=bool))
        scores = jnp.where(causal[None, None], scores, jnp.float32(-jnp.inf))
        attn = jax.nn.softmax(scores, axis=-1) * E ** (-0.5)
        o = jnp.einsum('bhts,bhsd->bhtd', attn, v)
        o = o.transpose(0, 2, 1, 3).reshape(B, T, E)
        return o @ w_proj + b_proj

    def _L0_ffn_ref(hidden_state, gate_w, gate_scale, up_w, up_scale, down_w, down_scale):
        import jax, jax.numpy as jnp
        import numpy as np
        ZERO_POINT = 128.0

        def _dequant(wq, scale):
            return (wq.astype(jnp.float32) - ZERO_POINT) * scale[:, None]
        Wg = _dequant(gate_w, gate_scale)
        Wu = _dequant(up_w, up_scale)
        Wd = _dequant(down_w, down_scale)
        g = jnp.einsum('bsh,ih->bsi', hidden_state, Wg)
        u = jnp.einsum('bsh,ih->bsi', hidden_state, Wu)
        h = jax.nn.silu(g) * u
        return jnp.einsum('bsi,hi->bsh', h, Wd)
    x = L0_attn_x
    xn = _layernorm(x, axis=-1)
    s = _L0_attn_ref(xn, L0_attn_w_attn, L0_attn_b_attn, L0_attn_w_proj, L0_attn_b_proj)
    g = _silu(_L0_ffn_ref(xn, L0_ffn_gate_w, L0_ffn_gate_scale, L0_ffn_up_w, L0_ffn_up_scale, L0_ffn_down_w, L0_ffn_down_scale))
    x = x + s * g
    return x

_drawn_inputs = setup_inputs


def setup_inputs(seed=0):
    import zlib

    import numpy as np

    out = dict(_drawn_inputs(seed))
    spreads = {'L0_attn_b_attn': (0.0, 0.1), 'L0_attn_b_proj': (0.0, 0.1)}
    factors = {}
    for name, (base, spread) in spreads.items():
        noise = np.random.default_rng([zlib.crc32(name.encode()), seed]).standard_normal(out[name].shape)
        drawn = base * np.exp(spread * noise) if base else spread * noise
        out[name] = jnp.asarray(drawn.astype(out[name].dtype))
    for name, factor in factors.items():
        out[name] = (out[name] * factor).astype(out[name].dtype)
    return out
```

```python
from contextlib import ExitStack

import concourse.bass as bass
from concourse import mybir
from concourse.alu_op_type import AluOpType as ALU

ACT = mybir.ActivationFunctionType
AX = mybir.AxisListType
F32 = mybir.dt.float32
BF16 = mybir.dt.bfloat16
I32 = mybir.dt.int32

P = 128
B, T, E = 4, 1024, 256
H, D = 16, 16
I = 1024
KT = E // P
GH = 4
SLOTS = H // GH
CH = 512
NC = T // CH
NJ = T // P
STEPS = [(c, j) for c in range(NC) for j in range((c + 1) * CH // P)]
NSTEP = len(STEPS)
NPOS = NSTEP * GH
MX_TILES = [(c, i, h) for c in range(NC) for i in range(c * CH // P, NJ) for h in range(GH)]
NMX = len(MX_TILES)
MX_FROM = 4
TERMS = 6
KROWS = TERMS * D
PARTS = 3
CPARTS = 2
UNITS = 4
PR = 3
LOWEST = -3.0e38
NEWTON = 3
LN_STEPS = NJ + 4 + 3 * NEWTON
EPS = 1e-5
ZERO_POINT = 128.0
RSQRT_GUESS = 0x5F3759DF
BANK_ST, BANK_MX, BANK_PV, BANK_G, BANK_U, BANK_X = 0, 2, 4, 5, 6, 7


def diagonal(k):
    c, j = STEPS[k]
    return j * P >= c * CH


def step_tokens(k):
    c, j = STEPS[k]
    first = max(c * CH, j * P)
    return first, (c + 1) * CH - first


def mx_of(pos):
    n = NPOS - MX_FROM * GH
    at = pos - MX_FROM * GH
    if at < 0:
        return range(0)
    return range(NMX * at // n, NMX * (at + 1) // n)


class Turn:

    def __init__(self, engine, turn, per=1, more=0, products=None):
        self.engine, self.turn, self.per, self.more = engine, turn, per, more
        self.products = {1: turn} if products is None else products

    def __add__(self, n):
        return Turn(self.engine, self.turn, self.per, self.more + n, self.products)

    def __sub__(self, n):
        return self + -n

    def __mul__(self, n):
        return Turn(self.engine, self.turn, self.per * n, self.more * n, self.products)

    __radd__, __rmul__ = __add__, __mul__


def count(n):
    if not isinstance(n, Turn):
        return n
    if n.per not in n.products:
        n.products[n.per] = n.engine.snap(n.turn * n.per)
    product = n.products[n.per]
    return product + n.more if n.more else product


def build(nc, x, w_attn, b_attn, w_proj, b_proj, gate_w, gate_scale, up_w, up_scale, down_w, down_scale,
          rope_cos, rope_sin, out):
    nc.disable_value_cache = True
    ctx = ExitStack()
    with ctx:
        def sb(name, shape, dt=F32):
            return ctx.enter_context(nc.sbuf_tensor(name, shape, dt))

        def sem(name):
            return ctx.enter_context(nc.semaphore(name))

        ident = sb("ident", [P, P])
        identb = sb("identb", [P, P], BF16)
        one = sb("one", [1, 2])
        causal = sb("causal", [P, CH], BF16)
        wa = sb("wa", [P, KT, 3 * E])
        ba = sb("ba", [1, 3 * E])
        wqk = sb("wqk", [P, KT, SLOTS, P])
        bqk_row = sb("bqk_row", [1, SLOTS, P])
        bqk = sb("bqk", [P, SLOTS])
        bv = sb("bv", [P, E])
        wp = sb("wp", [P, SLOTS, E])
        bp = sb("bp", [P, KT])
        wg = sb("wg", [P, KT, I])
        wu = sb("wu", [P, KT, I])
        wd = sb("wd", [P, I // P, E])
        gsc = sb("gsc", [P, I // P])
        usc = sb("usc", [P, I // P])
        dsc = sb("dsc", [P, KT])
        gsh = sb("gsh", [P, I // P])
        gus = sb("gus", [P, I // P])
        dsh = sb("dsh", [P, KT])
        xin = sb("xin", [P, NJ, E])
        stats = sb("stats", [P, NJ, 6])
        mv = sb("mv", [P, NJ, 2])
        nv = sb("nv", [P, 4, NJ])
        xn = sb("xn", [P, NJ, E])
        xnT = sb("xnT", [P, KT, T])
        xnT1 = sb("xnT1", [P, KT, CH])
        qf = sb("qf", [P, NC, CH])
        qks = sb("qks", [P, PARTS, T], BF16)
        qs = [sb(f"qs{i}", [KROWS + CPARTS, GH, T], BF16) for i in range(2)]
        ks = [sb(f"ks{i}", [KROWS + CPARTS, GH, T], BF16) for i in range(2)]
        vaug = sb("vaug", [P, NJ, H, 2 * D])
        junk = sb("junk", [P, 2, CH], BF16)
        mx = sb("mx", [P, GH, NJ])
        cs = sb("cs", [P, CPARTS, GH * NJ], BF16)
        ct = sb("ct", [CPARTS * GH * NJ, P], BF16)
        prob = sb("prob", [P, PR, GH, CH])
        quant = [prob[:, i, :, :].rearrange("p h c -> p (h c)").bitcast(I32) for i in range(3)]
        gi, ui = (quant[i].rearrange("p (n h) -> p n h", h=E) for i in range(2))
        di = quant[2].rearrange("p (k i) -> p k i", i=I)
        th = sb("th", [P, CH])
        gated = sb("gated", [P, CH])
        hid = sb("hid", [P, UNITS, CH])
        gacc = sb("gacc", [P, KT, T])
        tg = sb("tg", [P, KT, CH])
        osb = sb("osb", [P, CH])
        sumb = sb("sumb", [P, CH])
        rsum = sb("rsum", [P, CH])
        oT = sb("oT", [P, SLOTS, T])
        flat_o = oT[:, :, :].rearrange("p s t -> p (s t)")
        cosr, sinr = flat_o[:, 0:2 * E], flat_o[:, 2 * E:4 * E]
        rtmp = flat_o[:, 4 * E:10 * E].rearrange("p (r n) -> p r n", r=3)
        rtmp2 = flat_o[:, 10 * E:16 * E].rearrange("p (r n) -> p r n", r=3)
        z = xn[:, :, :].rearrange("p i e -> p (i e)").rearrange("p (k t) -> p k t", k=KT)
        bank = [ctx.enter_context(nc.psum_tensor(f"bank{i}", [P, CH], F32)) for i in range(8)]
        scratch = nc.dram_tensor("qk_parts", (2, P, PARTS, T), BF16, kind="Internal").ap()

        w_in = sem("w_in")
        consts = sem("consts")
        wp_zeroed = sem("wp_zeroed")
        pool_step = sem("pool_step")
        credit = sem("credit")
        w_conv = sem("w_conv")
        rope_step = sem("rope_step")
        rope_done = sem("rope_done")
        setup_tp = sem("setup_tp")
        setup_ev = sem("setup_ev")
        bias_tp = sem("bias_tp")
        bias_ev = sem("bias_ev")
        x_in = sem("x_in")
        xres_in = sem("xres_in")
        ln_step = sem("ln_step")
        xn_done = sem("xn_done")
        lt_done = sem("lt_done")
        lt_read = sem("lt_read")
        x1_in = sem("x1_in")
        p_done = sem("p_done")
        p_read = sem("p_read")
        hi_done = sem("hi_done")
        rest_done = sem("rest_done")
        mid_done = sem("mid_done")
        split_done = sem("split_done")
        qks_out = sem("qks_out")
        stack_in = [sem(f"stack_in{i}") for i in range(2)]
        v_done = sem("v_done")
        v_read = sem("v_read")
        mx_done = sem("mx_done")
        mx_read = sem("mx_read")
        cs_step = sem("cs_step")
        cs_done = sem("cs_done")
        ct_done = sem("ct_done")
        ct_read = sem("ct_read")
        ct_in = sem("ct_in")
        st_done = sem("st_done")
        exp_done = sem("exp_done")
        mask_done = sem("mask_done")
        pv_done = sem("pv_done")
        o_read = sem("o_read")
        sum_done = sem("sum_done")
        rsum_done = sem("rsum_done")
        on_done = sem("on_done")
        g_done = sem("g_done")
        th_done = sem("th_done")
        g_read = sem("g_read")
        u_done = sem("u_done")
        h_done = sem("h_done")
        dn_done = sem("dn_done")
        dn_read = sem("dn_read")
        tg_done = sem("tg_done")
        gate_done = sem("gate_done")
        pj_done = sem("pj_done")
        z_done = sem("z_done")
        zt_done = sem("zt_done")
        zt_read = sem("zt_read")
        out_done = sem("out_done")
        held_dve, held_pe, held_pool, held_sp = (sem(f"held_{e}") for e in ("dve", "pe", "pool", "sp"))

        EXP0, MXR0, PV0, O0, ZT0 = 2, 2, PR, 1, 4
        block = ctx.enter_context(nc.Block())

        def load_x(sp, b):
            sp.dma_start(xin[:, :, :], x[bass.ds(count(b), 1), :, :].rearrange("o (i p) e -> p (o i) e", p=P)).then_inc(x_in, 16)

        def load_stack(sp, g, par, wait_readers):
            sp.wait_ge(split_done, count(NC * (g + 1)))
            sp.dma_start(scratch[par], qks[:, :, :]).then_inc(qks_out, 16)
            sp.wait_ge(qks_out, count(16 * (g + 1)))
            if wait_readers:
                sp.wait_ge(st_done, count(NPOS * (g - 1)))
                sp.wait_ge(mx_done, count(NMX * (g - 1)))
            for side, dst in ((0, qs[par]), (1, ks[par])):
                parts = scratch[par, side * GH * D:(side + 1) * GH * D].rearrange("(h d) a t -> a d h t", h=GH)
                for row, reps in ((0, 3), (3, 2), (5, 1)):
                    n = row * D
                    if side == 1:
                        src = parts[0:reps]
                    else:
                        a = 3 - reps
                        src = parts[a:a + 1].broadcast_to([reps, D, GH, T])
                    for r in range(reps):
                        sp.dma_start(dst[n + r * D:n + (r + 1) * D, :, :], src[r]).then_inc(stack_in[par], 16)

        def load_shift(sp, g, par):
            sp.wait_ge(ct_read, count(g + 1))
            for a in range(CPARTS):
                sp.dma_start(qs[par][KROWS + a:KROWS + a + 1, :, :].rearrange("o h (i c) -> o (h i) c", c=P),
                             ct[a * GH * NJ:(a + 1) * GH * NJ, :]).then_inc(ct_in, 16)

        def keep_x1(sp, b):
            sp.wait_ge(u_done, count(UNITS * SLOTS * b))
            sp.wait_ge(lt_read, count(4 * (b + 1)))
            sp.dma_start(xnT1[:, :, :], xnT[:, :, CH:T]).then_inc(x1_in, 16)

        def sp_batch(sp, b, last):
            if not last:
                sp.wait_ge(xn_done, count(NJ * (b + 1)))
                sp.sem_inc(held_sp, 1)
                sp.wait_ge(out_done, count(16 * 4 * b))
                sp.sem_inc(held_sp, 1)
                load_x(sp, b + 1)
            keep_x1(sp, b)
            for s in range(SLOTS):
                g = SLOTS * b + s
                if s == 2:
                    if not last:
                        sp.wait_ge(xn_done, count(NJ * (b + 2)))
                    else:
                        sp.wait_ge(out_done, count(16 * 4 * b))
                    sp.sem_inc(held_sp, 1)
                    sp.dma_start(xin[:, :, :], x[bass.ds(count(b), 1), :, :].rearrange("o (i p) e -> p (o i) e", p=P)).then_inc(xres_in, 16)
                if not (last and s == SLOTS - 1):
                    load_shift(sp, g + 1, (s + 1) % 2)
                if not (last and s >= SLOTS - 2):
                    load_stack(sp, g + 2, s % 2, True)
            for u in range(4):
                sp.wait_ge(zt_read, count(ZT0 + 4 * b + u + 1))
                sp.sem_inc(held_sp, 1)
                sp.dma_start(out[bass.ds(count(b), 1), 2 * u * P:2 * (u + 1) * P, :].rearrange("o (i p) e -> p (o i) e", p=P),
                             xin[:, 2 * u:2 * u + 2, :]).then_inc(out_done, 16)

        @block.sync
        def _(sp):
            load_x(sp, 0)
            sp.dma_start(wa[:, :, :], w_attn.rearrange("(k p) n -> p k n", p=P)).then_inc(w_in, 16)
            sp.dma_start(ba[:, :], b_attn.rearrange("(o n) -> o n", o=1)).then_inc(w_in, 16)
            sp.dma_start(bv[:, :], b_attn[2 * E:3 * E].rearrange("(o n) -> o n", o=1).broadcast_to([P, E])).then_inc(w_in, 16)
            sp.dma_start(cosr, rope_cos.broadcast_to([P, 2 * E])).then_inc(w_in, 16)
            sp.dma_start(sinr, rope_sin.broadcast_to([P, 2 * E])).then_inc(w_in, 16)
            sp.wait_ge(wp_zeroed, 1)
            for q in range(GH):
                sp.dma_start(wp[32 * q:32 * q + D, :, :], w_proj.rearrange("(s q d) n -> q d s n", s=SLOTS, q=GH)[q]).then_inc(w_in, 16)
            sp.dma_start(bp[:, :], b_proj.rearrange("(k p) -> p k", p=P), allow_slow_non_contiguous=True).then_inc(w_in, 16)
            sp.dma_start(gsc[:, :], gate_scale.rearrange("(n p) -> p n", p=P), allow_slow_non_contiguous=True).then_inc(w_in, 16)
            sp.dma_start(usc[:, :], up_scale.rearrange("(n p) -> p n", p=P), allow_slow_non_contiguous=True).then_inc(w_in, 16)
            sp.dma_start(dsc[:, :], down_scale.rearrange("(n p) -> p n", p=P), allow_slow_non_contiguous=True).then_inc(w_in, 16)
            sp.dma_start(gi, gate_w.rearrange("(n p) h -> p n h", p=P)).then_inc(w_in, 16)
            sp.dma_start(ui, up_w.rearrange("(n p) h -> p n h", p=P)).then_inc(w_in, 16)
            sp.dma_start(di, down_w.rearrange("(n p) h -> p n h", p=P)).then_inc(w_in, 16)
            load_stack(sp, 0, 0, False)
            load_stack(sp, 1, 1, False)
            load_shift(sp, 0, 0)
            with sp.Fori(0, B - 1) as b:
                sp_batch(sp, Turn(sp, b), False)
            sp_batch(sp, B - 1, True)
            sp.wait_ge(out_done, count(16 * 4 * B))

        def pool_rest(pool, g):
            for c in range(NC):
                pool.wait_ge(hi_done, count(NC * g + c + 1))
                nc.gpsimd.tensor_tensor(qf[:, c, :], qf[:, c, :], qks[:, 0, c * CH:(c + 1) * CH], ALU.subtract).then_inc(rest_done, 1)

        def pool_norm(pool, b, s, c):
            w = NC * (SLOTS * b + s) + c
            pool.wait_ge(rsum_done, count(w + 1))
            pool.wait_ge(o_read, count(O0 + w + 1))
            pool.wait_ge(pj_done, count(4 * b))
            nc.gpsimd.tensor_tensor(oT[:, s, c * CH:(c + 1) * CH], osb[:, :], rsum[:, :], ALU.mult).then_inc(on_done, 1)

        def pool_batch(pool, b, last):
            for s in range(SLOTS):
                g = SLOTS * b + s
                for k in range(NSTEP):
                    if diagonal(k):
                        pool.wait_ge(exp_done, count(EXP0 + NPOS * g + GH * (k + 1)))
                        own = prob[:, k % PR, :, 0:P]
                        pool.sem_inc(held_pool, 1)
                        nc.gpsimd.affine_select(out=own, in_=own, compare_op=ALU.is_ge, fill=0.0, base=0,
                                                pattern=[[0, GH], [1, P]], channel_multiplier=-1).then_inc(mask_done, 1)
                    if k == 7:
                        pool_norm(pool, b, s, 0)
                if not (last and s >= SLOTS - 2):
                    pool_rest(pool, g + 2)
                pool_norm(pool, b, s, 1)

        @block.gpsimd
        def _(pool):
            nc.gpsimd.memset(wp[:, :, :], 0.0).then_inc(wp_zeroed, 1)
            nc.gpsimd.memset(ident[:, :], 0.0).then_inc(pool_step, 1)
            nc.gpsimd.memset(causal[:, :], 0.0).then_inc(pool_step, 1)
            nc.gpsimd.memset(one[:, :], 1.0).then_inc(consts, 1)
            pool.wait_ge(pool_step, 2)
            nc.gpsimd.affine_select(out=ident[:, :], in_=ident[:, :], compare_op=ALU.not_equal, fill=1.0,
                                    base=0, pattern=[[-1, P]], channel_multiplier=1).then_inc(pool_step, 1)
            nc.gpsimd.affine_select(out=causal[:, CH - P:CH], in_=causal[:, CH - P:CH], compare_op=ALU.is_ge, fill=LOWEST,
                                    base=0, pattern=[[-1, P]], channel_multiplier=1).then_inc(consts, 1)
            pool.wait_ge(pool_step, 3)
            nc.gpsimd.tensor_copy(identb[:, :], ident[:, :]).then_inc(consts, 1)
            pool_rest(pool, 0)
            pool_rest(pool, 1)
            with pool.Fori(0, B - 1) as b:
                pool_batch(pool, Turn(pool, b), False)
            pool_batch(pool, B - 1, True)

        N_CONSTS = 6

        def act_lt(act, b, u):
            k, half = u // 2, u % 2
            act.wait_ge(lt_done, count(4 * b + u + 1))
            nc.scalar.activation(xnT[:, k, half * CH:(half + 1) * CH], bank[BANK_X][:, :], ACT.Copy).then_inc(lt_read, 1)

        def act_p(act, g, s, c):
            act.wait_ge(p_done, count(NC * g + c + 1))
            act.wait_ge(split_done, count(NC * g))
            nc.scalar.activation(qf[:, c, :], bank[BANK_G + c][:, :], ACT.Identity, bias=bqk[:, s:s + 1]).then_inc(p_read, 1)

        def act_ct(act, g):
            act.wait_ge(ct_done, count(g + 1))
            act.wait_ge(ct_in, count(16 * CPARTS * g))
            nc.scalar.activation(ct[:, :], bank[BANK_X][:, :].bitcast(BF16)[0:CPARTS * GH * NJ, 0:P], ACT.Copy).then_inc(ct_read, 1)

        def act_o(act, g, c):
            w = NC * g + c
            act.wait_ge(pv_done, count(PV0 + NSTEP * g + (4 if c == 0 else NSTEP)))
            act.wait_ge(on_done, count(w))
            nc.scalar.activation(osb[:, :], bank[BANK_PV][:, :], ACT.Copy).then_inc(o_read, 1)

        def act_batch(act, b, last):
            for s in range(SLOTS):
                g = SLOTS * b + s
                for k in range(NSTEP):
                    _, n = step_tokens(k)
                    for h in range(GH):
                        i = GH * k + h
                        act.wait_ge(st_done, count(NPOS * g + i + 1))
                        if h == 0:
                            act.wait_ge(pv_done, count(NSTEP * g + k + 1))
                        nc.scalar.activation(prob[:, k % PR, h, 0:n], bank[BANK_ST + i % 2][:, 0:n], ACT.Exp).then_inc(exp_done, 1)
                        if k % 3 == 1 and h == 1:
                            n_u = UNITS * g + k // 3
                            act.wait_ge(g_done, count(n_u + 1))
                            act.wait_ge(g_read, count(n_u))
                            t = UNITS * (s % 2) + k // 3
                            nc.scalar.activation(th[:, :], bank[BANK_G][:, :], ACT.Tanh, scale=gsh[:, t:t + 1]).then_inc(th_done, 1)
                        if k == 5 and h == 2:
                            act_o(act, g, 0)
                        if s == 2 and not last and k % 3 == 2 and h == 0:
                            if k == 2:
                                act.wait_ge(p_done, count(NC * SLOTS * (b + 1)))
                                act.wait_ge(v_done, count(4 * (b + 1)))
                                act.wait_ge(u_done, count(UNITS * (SLOTS * b + 2)))
                                act.wait_ge(x1_in, count(16 * (b + 1)))
                            act_lt(act, b + 1, k // 3)
                if not (last and s >= SLOTS - 2):
                    act_p(act, g + 2, (s + 2) % SLOTS, 0)
                if not (last and s == SLOTS - 1):
                    act_ct(act, g + 1)
                act_o(act, g, 1)
                if not (last and s >= SLOTS - 2):
                    act_p(act, g + 2, (s + 2) % SLOTS, 1)
                if s % 2 == 1:
                    c = s // 2
                    for m in range(KT):
                        act.wait_ge(dn_read, count(KT * g + m + 1))
                        act.wait_ge(gate_done, count(4 * b + KT * c))
                        nc.scalar.activation(tg[:, m, :], gacc[:, m, c * CH:(c + 1) * CH], ACT.Tanh).then_inc(tg_done, 1)

        @block.scalar
        def _(act):
            for u in range(12):
                act.wait_ge(setup_tp, count(u + 1))
                if u < 8:
                    w, k, half = (wg, wu)[u // 4], (u % 4) // 2, u % 2
                    dst = w[:, k, half * CH:(half + 1) * CH]
                else:
                    dst = wd[:, 2 * (u - 8):2 * (u - 8) + 2, :]
                nc.scalar.activation(dst, bank[u % 4][:, :], ACT.Copy).then_inc(setup_ev, 1)
            for u in range(4):
                act_lt(act, 0, u)
            act.wait_ge(bias_tp, 1)
            nc.scalar.activation(bqk[:, :], bank[BANK_PV][:, 0:SLOTS], ACT.Copy).then_inc(bias_ev, 1)
            act.wait_ge(bias_ev, 1)
            for g in range(2):
                for c in range(NC):
                    act_p(act, g, g, c)
            act_ct(act, 0)
            act.wait_ge(credit, 5)
            with act.Fori(0, B - 1) as b:
                act_batch(act, Turn(act, b), False)
            act_batch(act, B - 1, True)

        def pe_lt(pe, b, u):
            k, half = u // 2, u % 2
            for i in range(4):
                t = 4 * half + i
                mm = nc.tensor.transpose(bank[BANK_X][:, i * P:(i + 1) * P], xn[:, t, k * P:(k + 1) * P], ident[:, :])
            mm.then_inc(lt_done, 1)

        def pe_p(pe, s, c):
            for k in range(KT):
                mm = nc.tensor.matmul(bank[BANK_G + c][:, :], wqk[:, k, s, :], xnT[:, k, c * CH:(c + 1) * CH],
                                      start=(k == 0), stop=(k == KT - 1))
            mm.then_inc(p_done, 1)

        def pe_v(pe, u, dst):
            for i in range(2):
                t = 2 * u + i
                for k in range(KT):
                    mm = nc.tensor.matmul(dst[:, i * E:(i + 1) * E], xnT[:, k, t * P:(t + 1) * P], wa[:, k, 2 * E:3 * E],
                                          start=(k == 0), stop=(k == KT - 1))
            mm.then_inc(v_done, 1)

        def pe_mx(pe, g, m, par):
            c, i, h = MX_TILES[m]
            n = min((i + 1) * P - c * CH, CH)
            pe.wait_ge(mx_read, count(NMX * g + m + 1))
            nc.tensor.matmul(bank[BANK_MX + m % 2][:, 0:n], qs[par][0:KROWS, h, i * P:(i + 1) * P],
                             ks[par][0:KROWS, h, c * CH:c * CH + n], start=True, stop=True).then_inc(mx_done, 1)

        def pe_ct(pe, g):
            pe.wait_ge(cs_done, count(g + 1))
            pe.sem_inc(held_pe, 1)
            nc.tensor.transpose(bank[BANK_X][:, :].bitcast(BF16)[0:CPARTS * GH * NJ, 0:P],
                                cs[:, :, :].rearrange("p a n -> p (a n)"), identb[:, :]).then_inc(ct_done, 1)

        def pe_pv(pe, b, s, k):
            g = SLOTS * b + s
            c, j = STEPS[k]
            first, n = step_tokens(k)
            if k == 0 and s == 0:
                pe.wait_ge(v_read, count(NJ * (b + 1)))
            if j == 0:
                pe.wait_ge(o_read, count(NC * g + c + 1))
            if diagonal(k):
                pe.wait_ge(mask_done, count(8 * g + (k + 1 if c == 0 else k - 3)))
            else:
                pe.wait_ge(exp_done, count(EXP0 + NPOS * g + GH * (k + 1)))
            for h in range(GH):
                at = first - c * CH
                mm = nc.tensor.matmul(bank[BANK_PV][32 * h:32 * h + 32, at:at + n], vaug[:, j, GH * s + h, :],
                                      prob[:, k % PR, h, 0:n], start=(j == 0), stop=(at + P == CH and n == P),
                                      tile_position=(0, 32 * h), skip_group_check=True)
            mm.then_inc(pv_done, 1)

        def pe_down(pe, g, s, m):
            pe.wait_ge(h_done, count(UNITS * (g + 1)))
            for i in range(UNITS):
                t = UNITS * (s % 2) + i
                mm = nc.tensor.matmul(bank[BANK_G + m][:, :], wd[:, t, m * P:(m + 1) * P], hid[:, i, :],
                                      start=(i == 0), stop=(i == UNITS - 1))
            mm.then_inc(dn_done, 1)

        def pe_batch(pe, b, last):
            for s in range(SLOTS):
                g = SLOTS * b + s
                par = s % 2
                pe.wait_ge(ct_in, count(16 * CPARTS * (g + 1)))
                for k in range(NSTEP):
                    c, j = STEPS[k]
                    first, n = step_tokens(k)
                    if k == MX_FROM and not (last and s == SLOTS - 1):
                        turn = (SLOTS // 2) * b + (s + 1) // 2 + 1
                        pe.wait_ge(stack_in[(s + 1) % 2], count(16 * 2 * TERMS * turn))
                    for h in range(GH):
                        i = GH * k + h
                        pe.wait_ge(exp_done, count(NPOS * g + i + 1))
                        nc.tensor.matmul(bank[BANK_ST + i % 2][:, 0:n], ks[par][:, h, j * P:(j + 1) * P],
                                         qs[par][:, h, first:first + n], start=True, stop=True).then_inc(st_done, 1)
                        if not (last and s == SLOTS - 1):
                            for m in mx_of(i):
                                pe_mx(pe, g + 1, m, (s + 1) % 2)
                        if i % 3 == 0:
                            unit, f = i // 12, (i // 3) % 4
                            t = UNITS * (s % 2) + unit
                            w, dst, done, kt = (wg, bank[BANK_G], g_done, f) if f < 2 else (wu, bank[BANK_U], u_done, f - 2)
                            if f == 0:
                                if unit:
                                    pe.wait_ge(g_read, count(UNITS * g + unit))
                                elif s:
                                    pe.wait_ge(dn_read, count(KT * g))
                                else:
                                    pe.wait_ge(zt_read, count(4 * b + 3))
                            if f == 2:
                                if unit:
                                    pe.wait_ge(h_done, count(UNITS * g + unit))
                                elif s:
                                    pe.wait_ge(dn_read, count(KT * g))
                                else:
                                    pe.wait_ge(zt_read, count(4 * b + 4))
                            if s == 2 and unit == 0 and f == 0:
                                pe.wait_ge(x1_in, count(16 * (b + 1)))
                            rows = xnT[:, kt, 0:CH] if s < 2 else xnT1[:, kt, :]
                            mm = nc.tensor.matmul(dst[:, :], w[:, kt, t * P:(t + 1) * P], rows, start=(kt == 0), stop=(kt == KT - 1))
                            if kt == KT - 1:
                                mm.then_inc(done, 1)
                    if k:
                        pe_pv(pe, b, s, k - 1)
                    if s == 2 and not last and k % 3 == 1:
                        u = k // 3
                        if u == 0:
                            pe.wait_ge(xn_done, count(NJ * (b + 2)))
                            pe.wait_ge(ct_read, count(g + 1))
                        else:
                            pe.wait_ge(lt_read, count(4 * (b + 1) + u))
                        pe_lt(pe, b + 1, u)
                more = not (last and s >= SLOTS - 2)
                if more:
                    if s == 2:
                        pe.wait_ge(lt_read, count(4 * (b + 2)))
                    pe.wait_ge(g_read, count(UNITS * (g + 1)))
                    pe_p(pe, (s + 2) % SLOTS, 0)
                if not (last and s == SLOTS - 1):
                    pe.wait_ge(ct_read, count(g + 1))
                    if s == 0:
                        pe.wait_ge(zt_read, count(4 * b + 2))
                    if s == 2 and not last:
                        pe.wait_ge(lt_read, count(4 * (b + 2)))
                    pe_ct(pe, g + 1)
                pe_pv(pe, b, s, NSTEP - 1)
                pe.wait_ge(h_done, count(UNITS * (g + 1)))
                if more:
                    pe_p(pe, (s + 2) % SLOTS, 1)
                for m in range(KT):
                    if more:
                        pe.wait_ge(p_read, count(NC * (g + 2) + m + 1))
                    pe_down(pe, g, s, m)
            g = SLOTS * (b + 1) - 1
            if not last:
                for u, x_bank in enumerate((BANK_X, BANK_G, BANK_U, BANK_X)):
                    if u == 0:
                        pe.wait_ge(ct_read, count(g + 2))
                    if u in (1, 2):
                        pe.wait_ge(dn_read, count(KT * (g + 1)))
                    if u == 3:
                        pe.wait_ge(v_read, count(NJ * (b + 1) + 2))
                    pe_v(pe, u, bank[x_bank])
            for u, x_bank in enumerate((BANK_G, BANK_U, BANK_X, BANK_G)):
                c, m = u // 2, u % 2
                if u == 0:
                    pe.wait_ge(on_done, count(NC * (g + 1)))
                    pe.wait_ge(dn_read, count(KT * (g + 1)))
                if u < 3 and not last:
                    pe.wait_ge(v_read, count(NJ * (b + 1) + 2 * (u + 2)))
                if u == 2 and last:
                    pe.wait_ge(ct_read, count(g + 1))
                if u == 3:
                    pe.wait_ge(z_done, count(4 * b + 1))
                for k in range(SLOTS):
                    mm = nc.tensor.matmul(bank[x_bank][:, :], wp[:, k, m * P:(m + 1) * P], oT[:, k, c * CH:(c + 1) * CH],
                                          start=(k == 0), stop=(k == SLOTS - 1))
                mm.then_inc(pj_done, 1)
            for u, x_bank in enumerate((BANK_U, BANK_X, BANK_G, BANK_U)):
                pe.wait_ge(z_done, count(4 * b + min(u + 2, 4)))
                if u == 3:
                    pe.wait_ge(zt_read, count(ZT0 + 4 * b + 1))
                for i in range(2):
                    for m in range(KT):
                        t = 2 * u + i
                        mm = nc.tensor.transpose(bank[x_bank][:, i * E + m * P:i * E + (m + 1) * P],
                                                 z[:, m, t * P:(t + 1) * P], ident[:, :])
                mm.then_inc(zt_done, 1)

        @block.tensor
        def _(pe):
            pe.wait_ge(consts, N_CONSTS)
            for u in range(12):
                if u % 4 == 0:
                    pe.wait_ge(w_conv, count(u // 4 + 1))
                if u >= 4:
                    pe.wait_ge(setup_ev, count(u - 3))
                for i in range(4):
                    if u < 8:
                        src = (gi, ui)[u // 4][:, 4 * (u % 2) + i, ((u % 4) // 2) * P:((u % 4) // 2 + 1) * P]
                    else:
                        t, m = 2 * (u - 8) + i // 2, i % 2
                        src = di[:, m, t * P:(t + 1) * P]
                    mm = nc.tensor.transpose(bank[u % 4][:, i * P:(i + 1) * P], src.bitcast(F32), ident[:, :])
                mm.then_inc(setup_tp, 1)
            pe.wait_ge(xn_done, NJ)
            for u in range(4):
                if u:
                    pe.wait_ge(lt_read, u)
                pe_lt(pe, 0, u)
            pe.wait_ge(rope_done, 2)
            for s in range(SLOTS):
                mm = nc.tensor.matmul(bank[BANK_PV][:, s:s + 1], bqk_row[0:1, s, :], one[0:1, 0:1], start=True, stop=True)
            mm.then_inc(bias_tp, 1)
            pe.wait_ge(lt_read, 4)
            for g in range(2):
                for c in range(NC):
                    if g:
                        pe.wait_ge(p_read, count(c + 1))
                    pe_p(pe, g, c)
            for u, x_bank in enumerate((BANK_X, BANK_G, BANK_U, BANK_X)):
                if u in (1, 2):
                    pe.wait_ge(p_read, count(NC + u))
                if u == 3:
                    pe.wait_ge(v_read, 2)
                pe_v(pe, u, bank[x_bank])
            pe.wait_ge(setup_ev, 12)
            pe.wait_ge(credit, 5)
            pe.wait_ge(stack_in[0], count(16 * 2 * TERMS))
            for m in range(NMX):
                pe_mx(pe, 0, m, 0)
            pe.wait_ge(v_read, NJ)
            pe_ct(pe, 0)
            with pe.Fori(0, B - 1) as b:
                pe_batch(pe, Turn(pe, b), False)
            pe_batch(pe, B - 1, True)

        def dve_ln(dve, b):
            dve.wait_ge(x_in, count(16 * (b + 1)))
            dve.wait_ge(lt_done, count(4 * b))
            base = LN_STEPS * b
            for t in range(NJ):
                nc.vector.bn_stats(stats[:, t, :], xin[:, t, :]).then_inc(ln_step, 1)
            n = base + NJ
            dve.wait_ge(ln_step, count(n))
            dve.sem_inc(held_dve, 1)
            for t in range(NJ):
                op = nc.vector.bn_aggr(mv[:, t, :], stats[:, t, :])
            op.then_inc(ln_step, 1)
            dve.wait_ge(ln_step, count(n + 1))
            var, guess, r, tmp = (nv[:, i, :] for i in range(4))
            nc.vector.tensor_scalar(var, mv[:, :, 1], EPS, None, ALU.add).then_inc(ln_step, 1)
            dve.wait_ge(ln_step, count(n + 2))
            nc.vector.tensor_scalar(guess.bitcast(I32), var.bitcast(I32), 1, None, ALU.logical_shift_right).then_inc(ln_step, 1)
            dve.wait_ge(ln_step, count(n + 3))
            n = n + 3
            nc.vector.tensor_scalar(r.bitcast(I32), guess.bitcast(I32), -1.0, float(RSQRT_GUESS), ALU.mult, ALU.add).then_inc(ln_step, 1)
            for _ in range(NEWTON):
                dve.wait_ge(ln_step, count(n + 1))
                nc.vector.tensor_tensor(tmp, r, r, ALU.mult).then_inc(ln_step, 1)
                dve.wait_ge(ln_step, count(n + 2))
                nc.vector.scalar_tensor_tensor(out=tmp, in0=tmp, scalar=-0.5, in1=var, op0=ALU.mult, op1=ALU.mult).then_inc(ln_step, 1)
                dve.wait_ge(ln_step, count(n + 3))
                nc.vector.scalar_tensor_tensor(out=r, in0=tmp, scalar=1.5, in1=r, op0=ALU.add, op1=ALU.mult).then_inc(ln_step, 1)
                n = n + 3
            dve.wait_ge(ln_step, count(n + 1))
            for t in range(NJ):
                nc.vector.tensor_scalar(xn[:, t, :], xin[:, t, :], mv[:, t, 0:1], r[:, t:t + 1],
                                        ALU.subtract, ALU.mult).then_inc(xn_done, 1)

        def dve_split(dve, g):
            for c in range(NC):
                dve.wait_ge(p_read, count(NC * g + c + 1))
                if c == 0:
                    dve.wait_ge(qks_out, count(16 * g))
                nc.vector.tensor_copy(qks[:, 0, c * CH:(c + 1) * CH], qf[:, c, :]).then_inc(hi_done, 1)
            for c in range(NC):
                dve.wait_ge(rest_done, count(NC * g + c + 1))
                nc.vector.tensor_copy(qks[:, 1, c * CH:(c + 1) * CH], qf[:, c, :]).then_inc(mid_done, 1)
            for c in range(NC):
                dve.wait_ge(mid_done, count(NC * g + c + 1))
                nc.vector.tensor_tensor(qks[:, 2, c * CH:(c + 1) * CH], qf[:, c, :], qks[:, 1, c * CH:(c + 1) * CH],
                                        ALU.subtract).then_inc(split_done, 1)

        def dve_v(dve, b, u, x_bank):
            dve.wait_ge(v_done, count(4 * b + u + 1))
            for i in range(2):
                t = 2 * u + i
                nc.vector.tensor_tensor(vaug[:, t, :, 0:D], bank[x_bank][:, i * E:(i + 1) * E].rearrange("p (h d) -> p h d", h=H),
                                        bv[:, :].rearrange("p (h d) -> p h d", h=H), ALU.add).then_inc(v_read, 1)

        def dve_mx(dve, g, m):
            c, i, h = MX_TILES[m]
            n = min((i + 1) * P - c * CH, CH)
            src = bank[BANK_MX + m % 2][:, 0:n]
            dst = mx[:, h, i:i + 1]
            dve.wait_ge(mx_done, count(NMX * g + m + 1))
            if i * P < (c + 1) * CH:
                dve.wait_ge(mx_read, count(NMX * g + m + 1))
                if c:
                    dve.wait_ge(mx_read, count(MXR0 + NMX * g + (i * GH + h) + 1))
                dve.sem_inc(held_dve, 1)
                nc.vector.tensor_tensor_reduce(junk[:, m % 2, 0:n], src, causal[:, CH - n:CH], 1.0, dst if c else LOWEST,
                                               ALU.add, ALU.max, dst).then_inc(mx_read, 1)
            else:
                nc.vector.tensor_reduce(dst, src, AX.X, ALU.max).then_inc(mx_read, 1)

        def dve_cs(dve, g):
            dve.wait_ge(mx_read, count(MXR0 + NMX * (g + 1)))
            dve.wait_ge(ct_done, count(g))
            flat = mx[:, :, :].rearrange("p h i -> p (h i)")
            nc.vector.tensor_scalar(cs[:, 0, :], flat, -1.0, None, ALU.mult).then_inc(cs_step, 1)
            dve.wait_ge(cs_step, count(g + 1))
            nc.vector.scalar_tensor_tensor(out=cs[:, 1, :], in0=flat, scalar=-1.0, in1=cs[:, 0, :],
                                           op0=ALU.mult, op1=ALU.subtract).then_inc(cs_done, 1)

        def dve_sum(dve, g, c):
            w = NC * g + c
            dve.wait_ge(o_read, count(O0 + w + 1))
            dve.sem_inc(held_dve, 1)
            nc.vector.stream_shuffle(sumb[:, :], osb[:, :], [D] * 32).then_inc(sum_done, 1)
            dve.wait_ge(sum_done, count(w + 1))
            dve.wait_ge(on_done, count(w))
            nc.vector.reciprocal(rsum[:, :], sumb[:, :]).then_inc(rsum_done, 1)

        def dve_batch(dve, b, last):
            for s in range(SLOTS):
                g = SLOTS * b + s
                if s == 1 and not last:
                    dve.wait_ge(zt_done, count(4 * b))
                    dve_ln(dve, b + 1)
                for k in range(NSTEP):
                    for h in range(GH):
                        i = GH * k + h
                        if not (last and s == SLOTS - 1):
                            for m in mx_of(i):
                                dve_mx(dve, g + 1, m)
                        unit = k // 3
                        t = UNITS * (s % 2) + unit
                        if k % 3 == 1 and h == 3:
                            dve.wait_ge(th_done, count(UNITS * g + unit + 1))
                            dve.wait_ge(h_done, count(UNITS * g + unit))
                            nc.vector.scalar_tensor_tensor(out=gated[:, :], in0=th[:, :], scalar=1.0, in1=bank[BANK_G][:, :],
                                                           op0=ALU.add, op1=ALU.mult).then_inc(g_read, 1)
                        if k % 3 == 2 and h == 3:
                            dve.wait_ge(u_done, count(UNITS * g + unit + 1))
                            dve.wait_ge(g_read, count(UNITS * g + unit + 1))
                            if unit == 0:
                                dve.wait_ge(dn_done, count(KT * g))
                            nc.vector.scalar_tensor_tensor(out=hid[:, unit, :], in0=bank[BANK_U][:, :], scalar=gus[:, t:t + 1],
                                                           in1=gated[:, :], op0=ALU.mult, op1=ALU.mult).then_inc(h_done, 1)
                    if k == 6:
                        dve_sum(dve, g, 0)
                if not (last and s == SLOTS - 1):
                    dve_cs(dve, g + 1)
                if not (last and s >= SLOTS - 2):
                    dve_split(dve, g + 2)
                dve_sum(dve, g, 1)
                c = s // 2
                for m in range(KT):
                    dst = gacc[:, m, c * CH:(c + 1) * CH]
                    dve.wait_ge(dn_done, count(KT * g + m + 1))
                    if s % 2 == 0:
                        dve.wait_ge(z_done, count(4 * b))
                        nc.vector.tensor_scalar(dst, bank[BANK_G + m][:, :], dsh[:, m:m + 1], None, ALU.mult).then_inc(dn_read, 1)
                    else:
                        dve.wait_ge(dn_read, count(KT * g))
                        nc.vector.scalar_tensor_tensor(out=dst, in0=bank[BANK_G + m][:, :], scalar=dsh[:, m:m + 1], in1=dst,
                                                       op0=ALU.mult, op1=ALU.add).then_inc(dn_read, 1)
                if s % 2 == 1:
                    for m in range(KT):
                        dst = gacc[:, m, c * CH:(c + 1) * CH]
                        dve.wait_ge(tg_done, count(4 * b + KT * c + m + 1))
                        nc.vector.scalar_tensor_tensor(out=dst, in0=tg[:, m, :], scalar=1.0, in1=dst,
                                                       op0=ALU.add, op1=ALU.mult).then_inc(gate_done, 1)
            if not last:
                dve.wait_ge(pv_done, count(PV0 + NSTEP * SLOTS * (b + 1)))
                for u, x_bank in enumerate((BANK_X, BANK_G, BANK_U, BANK_X)):
                    dve_v(dve, b + 1, u, x_bank)
            for u, x_bank in enumerate((BANK_G, BANK_U, BANK_X, BANK_G)):
                c, m = u // 2, u % 2
                dve.wait_ge(pj_done, count(4 * b + u + 1))
                dve.wait_ge(gate_done, count(4 * b + KT * c + m + 1))
                dve.wait_ge(lt_done, count(4 * (b + 1 if last else b + 2)))
                nc.vector.scalar_tensor_tensor(out=z[:, m, c * CH:(c + 1) * CH], in0=bank[x_bank][:, :], scalar=bp[:, m:m + 1],
                                               in1=gacc[:, m, c * CH:(c + 1) * CH], op0=ALU.add, op1=ALU.mult).then_inc(z_done, 1)
            for u, x_bank in enumerate((BANK_U, BANK_X, BANK_G, BANK_U)):
                dve.wait_ge(zt_done, count(4 * b + u + 1))
                dve.wait_ge(xres_in, count(16 * (b + 1)))
                nc.vector.tensor_tensor(xin[:, 2 * u:2 * u + 2, :], bank[x_bank][:, :].rearrange("p (i e) -> p i e", i=2),
                                        xin[:, 2 * u:2 * u + 2, :], ALU.add).then_inc(zt_read, 1)

        @block.vector
        def _(dve):
            for par in range(2):
                nc.vector.memset(ks[par][KROWS:KROWS + CPARTS, :, :], 1.0).then_inc(consts, 1)
            nc.vector.memset(vaug[:, :, :, :], float(E) ** 0.5).then_inc(consts, 1)
            nc.vector.memset(junk[:, 0, 0:2], 0.0).then_inc(exp_done, EXP0)
            nc.vector.memset(junk[:, 0, 2:4], 0.0).then_inc(mx_read, MXR0)
            nc.vector.memset(junk[:, 0, 4:6], 0.0).then_inc(pv_done, PV0)
            nc.vector.memset(junk[:, 0, 6:8], 0.0).then_inc(o_read, O0)
            nc.vector.memset(junk[:, 0, 8:10], 0.0).then_inc(zt_read, ZT0)
            nc.vector.memset(junk[:, 0, 10:12], 0.0).then_inc(credit, 5)
            dve_ln(dve, 0)
            dve.wait_ge(w_in, count(16 * N_W_IN_ALL))
            for w in (gi, ui, di):
                nc.vector.tensor_scalar(w.bitcast(F32), w, -ZERO_POINT, None, ALU.add).then_inc(w_conv, 1)
            n = 0
            for src, r, rows in ((wa[:, 0, 0:2 * E], 0, P), (wa[:, 1, 0:2 * E], 1, P), (ba[:, 0:2 * E], 2, 1)):
                direct, cross = rtmp[0:rows, r, :], rtmp2[0:rows, r, :]
                even, odd = (src.rearrange("p (n two) -> p n two", two=2)[:, :, i] for i in range(2))
                s_even, s_odd = (sinr[0:rows, :].rearrange("p (n two) -> p n two", two=2)[:, :, i] for i in range(2))
                c_even, c_odd = (cross.rearrange("p (n two) -> p n two", two=2)[:, :, i] for i in range(2))
                nc.vector.tensor_tensor(direct, src, cosr[0:rows, :], ALU.mult).then_inc(rope_step, 1)
                nc.vector.tensor_tensor(c_even, odd, s_even, ALU.mult).then_inc(rope_step, 1)
                nc.vector.tensor_tensor(c_odd, even, s_odd, ALU.mult).then_inc(rope_step, 1)
                n += 3
                dve.wait_ge(rope_step, count(n))
                for side in range(2):
                    dst = wqk[:, r, :, side * 64:(side + 1) * 64] if r < KT else bqk_row[:, :, side * 64:(side + 1) * 64]
                    op = nc.vector.tensor_tensor(dst, direct[:, side * E:(side + 1) * E].rearrange("p (s n) -> p s n", s=SLOTS),
                                                 cross[:, side * E:(side + 1) * E].rearrange("p (s n) -> p s n", s=SLOTS), ALU.add)
                if r:
                    op.then_inc(rope_done, 1)
            nc.vector.tensor_scalar(gsh[:, :], gsc[:, :], 0.5, None, ALU.mult).then_inc(rope_step, 1)
            nc.vector.tensor_scalar(dsh[:, :], dsc[:, :], 0.5, None, ALU.mult).then_inc(rope_step, 1)
            dve.wait_ge(rope_step, count(n + 2))
            nc.vector.tensor_tensor(gus[:, :], gsh[:, :], usc[:, :], ALU.mult).then_inc(rope_step, 1)
            dve.wait_ge(rope_step, count(n + 3))
            dve_split(dve, 0)
            dve_split(dve, 1)
            dve.wait_ge(consts, N_CONSTS)
            for u, x_bank in enumerate((BANK_X, BANK_G, BANK_U, BANK_X)):
                dve_v(dve, 0, u, x_bank)
            for m in range(NMX):
                dve_mx(dve, 0, m)
            dve_cs(dve, 0)
            with dve.Fori(0, B - 1) as b:
                dve_batch(dve, Turn(dve, b), False)
            dve_batch(dve, B - 1, True)


N_W_IN_ALL = 5 + GH + 4 + 3

_INS = ['L0_attn_x', 'L0_attn_w_attn', 'L0_attn_b_attn', 'L0_attn_w_proj', 'L0_attn_b_proj', 'L0_ffn_gate_w',
        'L0_ffn_gate_scale', 'L0_ffn_up_w', 'L0_ffn_up_scale', 'L0_ffn_down_w', 'L0_ffn_down_scale']


def _rope_rows():
    import numpy as np

    freqs = np.float32(10000.0) ** (-(np.arange(0, D, 2, dtype=np.float32) / np.float32(D)))
    angle = np.outer(np.arange(H, dtype=np.float32), freqs.astype(np.float32)).astype(np.float32)
    cos, sin = np.cos(angle).astype(np.float32), np.sin(angle).astype(np.float32)
    cos = np.stack([cos, cos], -1).reshape(1, E)
    sin = np.stack([-sin, sin], -1).reshape(1, E)
    return np.concatenate([cos, cos], 1), np.concatenate([sin, sin], 1)


def kernel(**inputs):
    import numpy as _np
    import concourse.bacc as _bacc
    from concourse import mybir as _mybir
    from concourse.bass_utils import run_bass_kernel_spmd as _run

    nc = _bacc.Bacc("TRN2", target_bir_lowering=False, num_devices=1)
    arrays, args = {}, []
    rope_cos, rope_sin = _rope_rows()
    named = [(name, inputs[name]) for name in _INS] + [("rope_cos", rope_cos), ("rope_sin", rope_sin)]
    for name, a in named:
        a = _np.ascontiguousarray(a)
        arrays[f"in_{name}"] = a
        args.append(nc.dram_tensor(f"in_{name}", a.shape, _mybir.dt.from_np(a.dtype), kind="ExternalInput").ap())
    args.append(nc.dram_tensor("out_y", (B, T, E), F32, kind="ExternalOutput").ap())
    build(nc, *args)
    r = _run(nc, [arrays], core_ids=[0])
    return r.results[0]["out_y"]
```

```python
from contextlib import ExitStack

import concourse.bass as bass
from concourse import mybir
from concourse.alu_op_type import AluOpType as ALU

ACT = mybir.ActivationFunctionType
AX = mybir.AxisListType
F32 = mybir.dt.float32
BF16 = mybir.dt.bfloat16
I32 = mybir.dt.int32

P = 128
B, T, E = 4, 1024, 256
H, D = 16, 16
I = 1024
KT = E // P
GH = 4
SLOTS = H // GH
CH = 512
NC = T // CH
NJ = T // P
STEPS = [(c, j) for c in range(NC) for j in range((c + 1) * CH // P)]
NSTEP = len(STEPS)
NPOS = NSTEP * GH
MX_TILES = [(c, i, h) for c in range(NC) for i in range(c * CH // P, NJ) for h in range(GH)]
NMX = len(MX_TILES)
LT_STEPS = (4, 6, 8, 10)
BLK = 32
NBLK = CH // BLK
PAIRS = SLOTS // 2
TERMS = 6
KROWS = TERMS * D
PARTS = 3
CPARTS = 2
UNITS = 4
PR = 3
LOWEST = -3.0e38
NEWTON = 3
LN_STEPS = NJ + 4 + 3 * NEWTON
EPS = 1e-5
ZERO_POINT = 128.0
RSQRT_GUESS = 0x5F3759DF
BANK_ST, BANK_MX, BANK_PV, BANK_G, BANK_U, BANK_X = 0, 2, 4, 5, 6, 7


def diagonal(k):
    c, j = STEPS[k]
    return j * P >= c * CH


def step_tokens(k):
    c, j = STEPS[k]
    first = max(c * CH, j * P)
    return first, (c + 1) * CH - first


assert NMX == NPOS


class Turn:

    def __init__(self, engine, turn, per=1, more=0, products=None):
        self.engine, self.turn, self.per, self.more = engine, turn, per, more
        self.products = {1: turn} if products is None else products

    def __add__(self, n):
        return Turn(self.engine, self.turn, self.per, self.more + n, self.products)

    def __sub__(self, n):
        return self + -n

    def __mul__(self, n):
        return Turn(self.engine, self.turn, self.per * n, self.more * n, self.products)

    __radd__, __rmul__ = __add__, __mul__


def count(n):
    if not isinstance(n, Turn):
        return n
    if n.per not in n.products:
        n.products[n.per] = n.engine.snap(n.turn * n.per)
    product = n.products[n.per]
    return product + n.more if n.more else product


def build(nc, x, w_attn, b_attn, w_proj, b_proj, gate_w, gate_scale, up_w, up_scale, down_w, down_scale,
          rope_cos, rope_sin, out):
    nc.disable_value_cache = True
    ctx = ExitStack()
    with ctx:
        def sb(name, shape, dt=F32):
            return ctx.enter_context(nc.sbuf_tensor(name, shape, dt))

        def sem(name):
            return ctx.enter_context(nc.semaphore(name))

        ident = sb("ident", [P, P])
        identb = sb("identb", [P, P], BF16)
        one = sb("one", [1, 2])
        causal = sb("causal", [P, CH], BF16)
        wv = sb("wv", [P, KT, E])
        wqk = sb("wqk", [P, KT, SLOTS, P])
        bqk = sb("bqk", [P, SLOTS])
        bv = sb("bv", [P, E])
        wp = sb("wp", [P, PAIRS, E])
        bp = sb("bp", [P, E])
        wg = sb("wg", [P, KT, I])
        wu = sb("wu", [P, KT, I])
        wd = sb("wd", [P, I // P, E])
        gsc = sb("gsc", [P, I // P])
        usc = sb("usc", [P, I // P])
        dsc = sb("dsc", [P, E])
        gsh = sb("gsh", [P, I // P])
        gus = sb("gus", [P, I // P])
        xin = sb("xin", [P, NJ, E])
        stats = sb("stats", [P, NJ, 6])
        mv = sb("mv", [P, NJ, 2])
        nv = sb("nv", [P, 4, NJ])
        xn = sb("xn", [P, NJ, E])
        xnT = sb("xnT", [P, KT, T])
        xnF = sb("xnF", [P, KT, T])
        qf = sb("qf", [P, NC, CH])
        qks = sb("qks", [P, PARTS, T], BF16)
        qs = [sb(f"qs{i}", [KROWS + CPARTS, GH, T], BF16) for i in range(2)]
        ks = [sb(f"ks{i}", [KROWS + CPARTS, GH, T], BF16) for i in range(2)]
        vaug = sb("vaug", [P, NJ, H, 2 * D])
        junk = sb("junk", [P, 2, CH], BF16)
        mx = sb("mx", [P, GH, NJ])
        cs = sb("cs", [P, CPARTS, GH * NJ], BF16)
        ct = sb("ct", [CPARTS * GH * NJ, P], BF16)
        prob = sb("prob", [P, PR, GH, CH])
        quant = [prob[:, i, :, :].rearrange("p h c -> p (h c)").bitcast(I32) for i in range(3)]
        gi, ui = (quant[i].rearrange("p (n h) -> p n h", h=E) for i in range(2))
        di = quant[2].rearrange("p (k i) -> p k i", i=I)
        th = sb("th", [P, CH])
        gated = sb("gated", [P, CH])
        hid = sb("hid", [P, UNITS, CH])
        gacc = sb("gacc", [P, NJ, E])
        flat_g = gacc[:, :, :].rearrange("p k t -> p (k t)")
        wa = flat_g[:, 0:4 * E].rearrange("p (k n) -> p k n", k=KT)
        ba = flat_g[0:1, 4 * E:6 * E]
        bqk_row = flat_g[0:1, 6 * E:8 * E].rearrange("o (s n) -> o s n", s=SLOTS)
        tg = sb("tg", [P, KT, CH])
        osb = sb("osb", [P, CH])
        o_rows = sb("o_rows", [P, NBLK, BLK])
        rsum = sb("rsum", [P, NBLK])
        pair = sb("pair", [P, NC, NBLK, BLK])
        oT = sb("oT", [P, PAIRS, T])
        flat_h = hid[:, :, :].rearrange("p u t -> p (u t)")
        flat_o = oT[:, :, :].rearrange("p s t -> p (s t)")
        cosr, sinr = flat_h[:, 0:2 * E], flat_h[:, 2 * E:4 * E]
        rtmp = [flat_h[:, 4 * E:6 * E], flat_h[:, 6 * E:8 * E], flat_o[:, 6 * E:8 * E]]
        rtmp2 = [flat_o[:, 2 * r * E:2 * (r + 1) * E] for r in range(3)]
        z = xn
        bank = [ctx.enter_context(nc.psum_tensor(f"bank{i}", [P, CH], F32)) for i in range(8)]
        scratch = nc.dram_tensor("qk_parts", (2, P, PARTS, T), BF16, kind="Internal").ap()

        w_in = sem("w_in")
        consts = sem("consts")
        pool_step = sem("pool_step")
        credit = sem("credit")
        w_conv = sem("w_conv")
        rope_step = sem("rope_step")
        rope_done = sem("rope_done")
        setup_tp = sem("setup_tp")
        setup_ev = sem("setup_ev")
        wd_ev = sem("wd_ev")
        bias_tp = sem("bias_tp")
        bias_ev = sem("bias_ev")
        x_in = sem("x_in")
        xres_in = sem("xres_in")
        ln_step = sem("ln_step")
        xn_done = sem("xn_done")
        lt_done = sem("lt_done")
        lt_read = sem("lt_read")
        xf_in = [sem(f"xf_in{c}") for c in range(NC)]
        p_done = sem("p_done")
        p_read = sem("p_read")
        hi_done = sem("hi_done")
        rest_done = sem("rest_done")
        mid_done = sem("mid_done")
        split_done = sem("split_done")
        qks_out = sem("qks_out")
        q0_in, k0_in, qk1_in = ([sem(f"{n}_in{i}") for i in range(2)] for n in ("q0", "k0", "qk1"))
        v_done = sem("v_done")
        v_read = sem("v_read")
        mx_done = sem("mx_done")
        mx_read = sem("mx_read")
        cs_step = sem("cs_step")
        cs_done = sem("cs_done")
        ct_done = sem("ct_done")
        ct_read = sem("ct_read")
        ct_in = sem("ct_in")
        st_done = sem("st_done")
        exp_done = sem("exp_done")
        mask_done = sem("mask_done")
        pv_done = sem("pv_done")
        o_read = sem("o_read")
        o_turned = sem("o_turned")
        rsum_done = sem("rsum_done")
        on_done = sem("on_done")
        pair_done = sem("pair_done")
        g_done = sem("g_done")
        th_done = sem("th_done")
        g_read = sem("g_read")
        u_done = sem("u_done")
        h_done = sem("h_done")
        dn_done = sem("dn_done")
        dn_read = sem("dn_read")
        tg_done = sem("tg_done")
        gate_done = sem("gate_done")
        pj_done = sem("pj_done")
        z_done = sem("z_done")
        zg_done = sem("zg_done")
        y_done = sem("y_done")
        out_done = sem("out_done")
        held_dve, held_pe, held_pool, held_sp = (sem(f"held_{e}") for e in ("dve", "pe", "pool", "sp"))

        EXP0, MXR0, PV0, O0, PAIR0 = 2, 2, PR, 1, NC
        FREE = 1
        block = ctx.enter_context(nc.Block())

        def load_x(sp, b):
            sp.dma_start(xin[:, :, :], x[bass.ds(count(b), 1), :, :].rearrange("o (i p) e -> p (o i) e", p=P)).then_inc(x_in, 16)

        def store_parts(sp, g, par):
            sp.wait_ge(split_done, count(NC * (g + 1)))
            sp.dma_start(scratch[par], qks[:, :, :]).then_inc(qks_out, 16)
            sp.wait_ge(qks_out, count(16 * (g + 1)))

        def load_half(sp, par, side, c, done):
            dst = (qs, ks)[side][par]
            parts = scratch[par, side * GH * D:(side + 1) * GH * D].rearrange("(h d) a t -> a d h t", h=GH)
            for row, part in enumerate(((0, 0, 0, 1, 1, 2), (0, 1, 2, 0, 1, 0))[side]):
                sp.dma_start(dst[row * D:(row + 1) * D, :, c * CH:(c + 1) * CH],
                             parts[part, :, :, c * CH:(c + 1) * CH]).then_inc(done[par], 16)

        def load_shift(sp, g, par):
            sp.wait_ge(ct_read, count(g + 1))
            for a in range(CPARTS):
                sp.dma_start(qs[par][KROWS + a:KROWS + a + 1, :, :].rearrange("o h (i c) -> o (h i) c", c=P),
                             ct[a * GH * NJ:(a + 1) * GH * NJ, :]).then_inc(ct_in, 16)

        def keep_x(sp, c):
            sp.dma_start(xnF[:, :, c * CH:(c + 1) * CH], xnT[:, :, c * CH:(c + 1) * CH]).then_inc(xf_in[c], 16)

        def sp_batch(sp, b, last):
            if not last:
                sp.wait_ge(xn_done, count(NJ * (b + 1)))
                sp.sem_inc(held_sp, 1)
                sp.wait_ge(out_done, count(16 * 4 * b + FREE))
                sp.sem_inc(held_sp, 1)
                load_x(sp, b + 1)
            sp.wait_ge(u_done, count(UNITS * SLOTS * b + FREE))
            sp.wait_ge(lt_read, count(4 * (b + 1)))
            keep_x(sp, 1)
            for s in range(SLOTS):
                g = SLOTS * b + s
                par = s % 2
                if s == 2:
                    if not last:
                        sp.wait_ge(xn_done, count(NJ * (b + 2)))
                    else:
                        sp.wait_ge(out_done, count(16 * 4 * b + FREE))
                    sp.sem_inc(held_sp, 1)
                    sp.dma_start(xin[:, :, :], x[bass.ds(count(b), 1), :, :].rearrange("o (i p) e -> p (o i) e", p=P)).then_inc(xres_in, 16)
                    if not last:
                        sp.wait_ge(u_done, count(UNITS * (SLOTS * b + 2) + FREE))
                        sp.wait_ge(lt_read, count(4 * (b + 2)))
                        keep_x(sp, 0)
                more = not (last and s >= SLOTS - 2)
                if more:
                    store_parts(sp, g + 2, par)
                    sp.wait_ge(st_done, count(NPOS * g + GH * 4))
                    load_half(sp, par, 0, 0, q0_in)
                    sp.wait_ge(st_done, count(NPOS * g + GH * 8))
                    load_half(sp, par, 1, 0, k0_in)
                if not (last and s == SLOTS - 1):
                    load_shift(sp, g + 1, 1 - par)
                if more:
                    sp.wait_ge(st_done, count(NPOS * (g + 1)))
                    load_half(sp, par, 0, 1, qk1_in)
                    load_half(sp, par, 1, 1, qk1_in)
            for u in range(4):
                sp.wait_ge(y_done, count(4 * b + u + 1 + FREE))
                sp.sem_inc(held_sp, 1)
                sp.dma_start(out[bass.ds(count(b), 1), 2 * u * P:2 * (u + 1) * P, :].rearrange("o (i p) e -> p (o i) e", p=P),
                             xin[:, 2 * u:2 * u + 2, :]).then_inc(out_done, 16)

        @block.sync
        def _(sp):
            load_x(sp, 0)
            sp.dma_start(wa, w_attn[:, 0:2 * E].rearrange("(k p) n -> p k n", p=P)).then_inc(w_in, 16)
            sp.dma_start(wv[:, :, :], w_attn[:, 2 * E:3 * E].rearrange("(k p) n -> p k n", p=P)).then_inc(w_in, 16)
            sp.dma_start(ba, b_attn[0:2 * E].rearrange("(o n) -> o n", o=1)).then_inc(w_in, 16)
            sp.dma_start(bv[:, :], b_attn[2 * E:3 * E].rearrange("(o n) -> o n", o=1).broadcast_to([P, E])).then_inc(w_in, 16)
            sp.dma_start(cosr, rope_cos.broadcast_to([P, 2 * E])).then_inc(w_in, 16)
            sp.dma_start(sinr, rope_sin.broadcast_to([P, 2 * E])).then_inc(w_in, 16)
            for q in range(GH):
                for half in range(2):
                    sp.dma_start(wp[BLK * q + D * half:BLK * q + D * (half + 1), :, :],
                                 w_proj.rearrange("(t s q d) n -> q s d t n", t=PAIRS, s=2, q=GH)[q, half]).then_inc(w_in, 16)
            sp.dma_start(bp[:, :], b_proj.rearrange("(o n) -> o n", o=1).broadcast_to([P, E])).then_inc(w_in, 16)
            sp.dma_start(gsc[:, :], gate_scale.rearrange("(n p) -> p n", p=P), allow_slow_non_contiguous=True).then_inc(w_in, 16)
            sp.dma_start(usc[:, :], up_scale.rearrange("(n p) -> p n", p=P), allow_slow_non_contiguous=True).then_inc(w_in, 16)
            sp.dma_start(dsc[:, :], down_scale.rearrange("(o n) -> o n", o=1).broadcast_to([P, E])).then_inc(w_in, 16)
            sp.dma_start(gi, gate_w.rearrange("(n p) h -> p n h", p=P)).then_inc(w_in, 16)
            sp.dma_start(ui, up_w.rearrange("(n p) h -> p n h", p=P)).then_inc(w_in, 16)
            sp.dma_start(di, down_w.rearrange("(n p) h -> p n h", p=P)).then_inc(w_in, 16)
            sp.wait_ge(lt_read, 4)
            keep_x(sp, 0)
            for g in range(2):
                store_parts(sp, g, g)
                load_half(sp, g, 0, 0, q0_in)
                load_half(sp, g, 1, 0, k0_in)
                load_half(sp, g, 0, 1, qk1_in)
                load_half(sp, g, 1, 1, qk1_in)
            load_shift(sp, 0, 0)
            with sp.Fori(0, B - 1) as b:
                sp_batch(sp, Turn(sp, b), False)
            sp_batch(sp, B - 1, True)
            sp.wait_ge(out_done, count(16 * 4 * B + FREE))

        def pool_rest(pool, g, c):
            pool.wait_ge(hi_done, count(NC * g + c + 1))
            nc.gpsimd.tensor_tensor(qf[:, c, :], qf[:, c, :], qks[:, 0, c * CH:(c + 1) * CH], ALU.subtract).then_inc(rest_done, 1)

        def pool_norm(pool, b, s, c):
            w = NC * (SLOTS * b + s) + c
            pool.wait_ge(rsum_done, count(w + 1))
            if s % 2 == 0:
                pool.wait_ge(pair_done, count(NC * PAIRS * b + NC * (s // 2) + c + 1))
            nc.gpsimd.tensor_tensor(pair[:, c, :, D * (s % 2):D * (s % 2 + 1)], o_rows[:, :, 0:D],
                                    rsum[:, :].rearrange("p (n o) -> p n o", o=1).broadcast_to([P, NBLK, D]), ALU.mult).then_inc(on_done, 1)

        def pool_y(pool, b, u):
            pool.wait_ge(zg_done, count(4 * b + u + 1 + FREE))
            pool.wait_ge(xres_in, count(16 * (b + 1)))
            nc.gpsimd.tensor_tensor(xin[:, 2 * u:2 * u + 2, :], z[:, 2 * u:2 * u + 2, :], xin[:, 2 * u:2 * u + 2, :], ALU.add).then_inc(y_done, 1)

        def pool_batch(pool, b, last):
            for s in range(SLOTS):
                g = SLOTS * b + s
                for k in range(NSTEP):
                    if diagonal(k):
                        pool.wait_ge(exp_done, count(EXP0 + NPOS * g + GH * (k + 1)))
                        pool.sem_inc(held_pool, 1)
                        own = prob[:, k % PR, :, 0:P]
                        nc.gpsimd.affine_select(out=own, in_=own, compare_op=ALU.is_ge, fill=0.0, base=0,
                                                pattern=[[0, GH], [1, P]], channel_multiplier=-1).then_inc(mask_done, 1)
                    if k < NC and not (last and s >= SLOTS - 2):
                        pool_rest(pool, g + 2, k)
                    if k == 3 and s:
                        pool_norm(pool, b, s - 1, 1)
                    if k == 8:
                        pool_norm(pool, b, s, 0)
            pool_norm(pool, b, SLOTS - 1, 1)
            for u in range(4):
                pool_y(pool, b, u)

        @block.gpsimd
        def _(pool):
            nc.gpsimd.memset(ident[:, :], 0.0).then_inc(pool_step, 1)
            nc.gpsimd.memset(causal[:, :], 0.0).then_inc(pool_step, 1)
            nc.gpsimd.memset(one[:, :], 1.0).then_inc(consts, 1)
            pool.wait_ge(pool_step, 2)
            nc.gpsimd.affine_select(out=ident[:, :], in_=ident[:, :], compare_op=ALU.not_equal, fill=1.0,
                                    base=0, pattern=[[-1, P]], channel_multiplier=1).then_inc(pool_step, 1)
            nc.gpsimd.affine_select(out=causal[:, CH - P:CH], in_=causal[:, CH - P:CH], compare_op=ALU.is_ge, fill=LOWEST,
                                    base=0, pattern=[[-1, P]], channel_multiplier=1).then_inc(consts, 1)
            pool.wait_ge(pool_step, 3)
            nc.gpsimd.tensor_copy(identb[:, :], ident[:, :]).then_inc(consts, 1)
            for g in range(2):
                for c in range(NC):
                    pool_rest(pool, g, c)
            with pool.Fori(0, B - 1) as b:
                pool_batch(pool, Turn(pool, b), False)
            pool_batch(pool, B - 1, True)

        N_CONSTS = 6

        def act_lt(act, b, u):
            k, half = u // 2, u % 2
            act.wait_ge(lt_done, count(4 * b + u + 1))
            nc.scalar.activation(xnT[:, k, half * CH:(half + 1) * CH], bank[BANK_X][:, :], ACT.Copy).then_inc(lt_read, 1)

        def act_p(act, g, s, c):
            act.wait_ge(p_done, count(NC * g + c + 1))
            act.wait_ge(split_done, count(NC * g))
            nc.scalar.activation(qf[:, c, :], bank[BANK_G + c][:, :], ACT.Identity, bias=bqk[:, s:s + 1]).then_inc(p_read, 1)

        def act_ct(act, g):
            act.wait_ge(ct_done, count(g + 1))
            act.wait_ge(ct_in, count(16 * CPARTS * g))
            nc.scalar.activation(ct[:, :], bank[BANK_X][:, :].bitcast(BF16)[0:CPARTS * GH * NJ, 0:P], ACT.Copy).then_inc(ct_read, 1)

        def act_o(act, g, c):
            w = NC * g + c
            act.wait_ge(pv_done, count(PV0 + NSTEP * g + (4 if c == 0 else NSTEP)))
            act.wait_ge(o_turned, count(w + FREE))
            nc.scalar.activation(osb[:, :], bank[BANK_PV][:, :], ACT.Copy).then_inc(o_read, 1)

        def acc(c, m):
            t = c * CH // P + 2 * m
            return gacc[:, t:t + 2, :].rearrange("p i e -> p (i e)")

        def act_batch(act, b, last):
            for s in range(SLOTS):
                g = SLOTS * b + s
                for k in range(NSTEP):
                    _, n = step_tokens(k)
                    for h in range(GH):
                        i = GH * k + h
                        act.wait_ge(st_done, count(NPOS * g + i + 1))
                        if h == 0:
                            act.wait_ge(pv_done, count(NSTEP * g + k + 1))
                        nc.scalar.activation(prob[:, k % PR, h, 0:n], bank[BANK_ST + i % 2][:, 0:n], ACT.Exp).then_inc(exp_done, 1)
                        if k % 3 == 1 and h == 1:
                            n_u = UNITS * g + k // 3
                            act.wait_ge(g_done, count(n_u + 1))
                            act.wait_ge(g_read, count(n_u + FREE))
                            t = UNITS * (s % 2) + k // 3
                            nc.scalar.activation(th[:, :], bank[BANK_G][:, :], ACT.Tanh, scale=gsh[:, t:t + 1]).then_inc(th_done, 1)
                        if k == 5 and h == 2:
                            act_o(act, g, 0)
                        if s == 1 and not last and k in LT_STEPS and h == 3:
                            if k == LT_STEPS[0]:
                                act.wait_ge(p_done, count(NC * SLOTS * (b + 1)))
                                act.wait_ge(v_done, count(4 * (b + 1)))
                                act.wait_ge(xf_in[1], count(16 * (b + 1)))
                            act_lt(act, b + 1, LT_STEPS.index(k))
                more = not (last and s >= SLOTS - 3)
                if more:
                    act_p(act, g + 3, (s + 3) % SLOTS, 0)
                if not (last and s == SLOTS - 1):
                    act_ct(act, g + 1)
                act_o(act, g, 1)
                if more:
                    act_p(act, g + 3, (s + 3) % SLOTS, 1)
                if s % 2 == 1:
                    c = s // 2
                    for m in range(KT):
                        act.wait_ge(dn_read, count(KT * g + m + 1))
                        act.wait_ge(gate_done, count(4 * b + KT * c + FREE))
                        nc.scalar.activation(tg[:, m, :], acc(c, m), ACT.Tanh).then_inc(tg_done, 1)

        @block.scalar
        def _(act):
            for u in range(8):
                act.wait_ge(setup_tp, count(u + 1))
                w, k, half = (wg, wu)[u // 4], (u % 4) // 2, u % 2
                nc.scalar.activation(w[:, k, half * CH:(half + 1) * CH], bank[u % 4][:, :], ACT.Copy).then_inc(setup_ev, 1)
            for u in range(4):
                act_lt(act, 0, u)
            act.wait_ge(bias_tp, 1)
            nc.scalar.activation(bqk[:, :], bank[BANK_PV][:, 0:SLOTS], ACT.Copy).then_inc(bias_ev, 1)
            act.wait_ge(bias_ev, 1)
            for g in range(3):
                for c in range(NC):
                    act_p(act, g, g, c)
            act_ct(act, 0)
            act.wait_ge(credit, 5)
            with act.Fori(0, B - 1) as b:
                act_batch(act, Turn(act, b), False)
            act_batch(act, B - 1, True)

        def pe_lt(pe, b, u):
            k, half = u // 2, u % 2
            for i in range(4):
                t = 4 * half + i
                mm = nc.tensor.transpose(bank[BANK_X][:, i * P:(i + 1) * P], xn[:, t, k * P:(k + 1) * P], ident[:, :])
            mm.then_inc(lt_done, 1)

        def pe_p(pe, s, c):
            for k in range(KT):
                mm = nc.tensor.matmul(bank[BANK_G + c][:, :], wqk[:, k, s, :], xnT[:, k, c * CH:(c + 1) * CH],
                                      start=(k == 0), stop=(k == KT - 1))
            mm.then_inc(p_done, 1)

        def pe_v(pe, u, dst):
            for i in range(2):
                t = 2 * u + i
                for k in range(KT):
                    mm = nc.tensor.matmul(dst[:, i * E:(i + 1) * E], xnT[:, k, t * P:(t + 1) * P], wv[:, k, :],
                                          start=(k == 0), stop=(k == KT - 1))
            mm.then_inc(v_done, 1)

        def pe_mx(pe, g, m, par):
            c, i, h = MX_TILES[m]
            n = min((i + 1) * P - c * CH, CH)
            pe.wait_ge(mx_read, count(NMX * g + m + 1))
            nc.tensor.matmul(bank[BANK_MX + m % 2][:, 0:n], qs[par][0:KROWS, h, i * P:(i + 1) * P],
                             ks[par][0:KROWS, h, c * CH:c * CH + n], start=True, stop=True).then_inc(mx_done, 1)

        def pe_ct(pe, g):
            pe.wait_ge(cs_done, count(g + 1))
            pe.sem_inc(held_pe, 1)
            nc.tensor.transpose(bank[BANK_X][:, :].bitcast(BF16)[0:CPARTS * GH * NJ, 0:P],
                                cs[:, :, :].rearrange("p a n -> p (a n)"), identb[:, :]).then_inc(ct_done, 1)

        def pe_pv(pe, b, s, k):
            g = SLOTS * b + s
            c, j = STEPS[k]
            first, n = step_tokens(k)
            if k == 0 and s == 0:
                pe.wait_ge(v_read, count(NJ * (b + 1)))
            if j == 0:
                pe.wait_ge(o_read, count(NC * g + c + 1))
            if diagonal(k):
                pe.wait_ge(mask_done, count(8 * g + (k + 1 if c == 0 else k - 3)))
            else:
                pe.wait_ge(exp_done, count(EXP0 + NPOS * g + GH * (k + 1)))
            for h in range(GH):
                at = first - c * CH
                mm = nc.tensor.matmul(bank[BANK_PV][32 * h:32 * h + 32, at:at + n], vaug[:, j, GH * s + h, :],
                                      prob[:, k % PR, h, 0:n], start=(j == 0), stop=(at + P == CH and n == P),
                                      tile_position=(0, 32 * h), skip_group_check=True)
            mm.then_inc(pv_done, 1)

        def pe_down(pe, g, s, m):
            pe.wait_ge(h_done, count(UNITS * (g + 1) + FREE))
            for i in range(2):
                for unit in range(UNITS):
                    mm = nc.tensor.matmul(bank[BANK_G + m][:, i * E:(i + 1) * E], hid[:, unit, (2 * m + i) * P:(2 * m + i + 1) * P],
                                          wd[:, UNITS * (s % 2) + unit, :], start=(unit == 0), stop=(unit == UNITS - 1))
            mm.then_inc(dn_done, 1)

        def pe_batch(pe, b, last):
            for s in range(SLOTS):
                g = SLOTS * b + s
                par = s % 2
                pe.wait_ge(ct_in, count(16 * CPARTS * (g + 1)))
                for k in range(NSTEP):
                    c, j = STEPS[k]
                    first, n = step_tokens(k)
                    if not (last and s == SLOTS - 1):
                        turn = (SLOTS // 2) * b + (s + 1) // 2 + 1
                        if k == 0:
                            pe.wait_ge(q0_in[1 - par], count(16 * TERMS * turn))
                            pe.wait_ge(k0_in[1 - par], count(16 * TERMS * turn))
                        if k == 4:
                            pe.wait_ge(qk1_in[1 - par], count(16 * 2 * TERMS * turn))
                    for h in range(GH):
                        i = GH * k + h
                        pe.wait_ge(exp_done, count(NPOS * g + i + 1))
                        nc.tensor.matmul(bank[BANK_ST + i % 2][:, 0:n], ks[par][:, h, j * P:(j + 1) * P],
                                         qs[par][:, h, first:first + n], start=True, stop=True).then_inc(st_done, 1)
                        if not (last and s == SLOTS - 1):
                            pe_mx(pe, g + 1, i, 1 - par)
                        if i % 3 == 0:
                            unit, f = i // 12, (i // 3) % 4
                            t = UNITS * (s % 2) + unit
                            w, dst, done, kt = (wg, bank[BANK_G], g_done, f) if f < 2 else (wu, bank[BANK_U], u_done, f - 2)
                            if f == 0:
                                if unit:
                                    pe.wait_ge(g_read, count(UNITS * g + unit + FREE))
                                elif s:
                                    pe.wait_ge(dn_read, count(KT * g))
                                else:
                                    pe.wait_ge(z_done, count(4 * b + FREE))
                            if f == 2:
                                if unit:
                                    pe.wait_ge(h_done, count(UNITS * g + unit + FREE))
                                elif s:
                                    pe.wait_ge(dn_read, count(KT * g))
                                else:
                                    pe.wait_ge(z_done, count(4 * b + FREE))
                            if s % 2 == 0 and unit == 0 and f == 0:
                                pe.wait_ge(xf_in[s // 2], count(16 * (b + 1)))
                            rows = xnF[:, kt, (s // 2) * CH:(s // 2 + 1) * CH]
                            mm = nc.tensor.matmul(dst[:, :], w[:, kt, t * P:(t + 1) * P], rows, start=(kt == 0), stop=(kt == KT - 1))
                            if kt == KT - 1:
                                mm.then_inc(done, 1)
                    if k:
                        pe_pv(pe, b, s, k - 1)
                    if s == 1 and not last and k in LT_STEPS:
                        u = LT_STEPS.index(k)
                        if u == 0:
                            pe.wait_ge(xn_done, count(NJ * (b + 2)))
                            pe.wait_ge(ct_read, count(g + 1))
                        else:
                            pe.wait_ge(lt_read, count(4 * (b + 1) + u))
                        pe_lt(pe, b + 1, u)
                more = not (last and s >= SLOTS - 3)
                if more:
                    if s == 1:
                        pe.wait_ge(lt_read, count(4 * (b + 2)))
                    pe.wait_ge(g_read, count(UNITS * (g + 1) + FREE))
                    pe_p(pe, (s + 3) % SLOTS, 0)
                if not (last and s == SLOTS - 1):
                    pe.wait_ge(ct_read, count(g + 1))
                    if s == 0:
                        pe.wait_ge(z_done, count(4 * b + FREE))
                    if s == 1 and not last:
                        pe.wait_ge(lt_read, count(4 * (b + 2)))
                    pe_ct(pe, g + 1)
                pe_pv(pe, b, s, NSTEP - 1)
                pe.wait_ge(h_done, count(UNITS * (g + 1) + FREE))
                if more:
                    pe_p(pe, (s + 3) % SLOTS, 1)
                for m in range(KT):
                    if more:
                        pe.wait_ge(p_read, count(NC * (g + 3) + m + 1))
                    pe_down(pe, g, s, m)
            g = SLOTS * (b + 1) - 1
            if not last:
                for u, x_bank in enumerate((BANK_X, BANK_G, BANK_U, BANK_X)):
                    if u == 0:
                        pe.wait_ge(ct_read, count(g + 2))
                    if u in (1, 2):
                        pe.wait_ge(dn_read, count(KT * (g + 1)))
                    if u == 3:
                        pe.wait_ge(v_read, count(NJ * (b + 1) + 2))
                    pe_v(pe, u, bank[x_bank])
            for u, x_bank in enumerate((BANK_G, BANK_U, BANK_X, BANK_G)):
                if u == 0:
                    pe.wait_ge(dn_read, count(KT * (g + 1)))
                if u < 3 and not last:
                    pe.wait_ge(v_read, count(NJ * (b + 1) + 2 * (u + 2)))
                if u == 2 and last:
                    pe.wait_ge(ct_read, count(g + 1))
                if u == 3:
                    pe.wait_ge(z_done, count(4 * b + 1 + FREE))
                if u % 2 == 0:
                    pe.wait_ge(pair_done, count(PAIR0 + NC * PAIRS * (b + 1) - NC + u // 2 + 1))
                for i in range(2):
                    t = 2 * u + i
                    for k in range(PAIRS):
                        mm = nc.tensor.matmul(bank[x_bank][:, i * E:(i + 1) * E], oT[:, k, t * P:(t + 1) * P], wp[:, k, :],
                                              start=(k == 0), stop=(k == PAIRS - 1))
                mm.then_inc(pj_done, 1)

        @block.tensor
        def _(pe):
            pe.wait_ge(consts, N_CONSTS)
            for u in range(12):
                if u % 4 == 0:
                    pe.wait_ge(w_conv, count(u // 4 + 1))
                if u >= 4:
                    pe.wait_ge(setup_ev, u - 3)
                for i in range(4):
                    if u < 8:
                        src = (gi, ui)[u // 4][:, 4 * (u % 2) + i, ((u % 4) // 2) * P:((u % 4) // 2 + 1) * P]
                    else:
                        t, m = 2 * (u - 8) + i // 2, i % 2
                        src = di[:, m, t * P:(t + 1) * P]
                    mm = nc.tensor.transpose(bank[u % 4][:, i * P:(i + 1) * P], src.bitcast(F32), ident[:, :])
                mm.then_inc(setup_tp, 1)
            pe.wait_ge(xn_done, NJ)
            for u in range(4):
                if u:
                    pe.wait_ge(lt_read, u)
                pe_lt(pe, 0, u)
            pe.wait_ge(rope_done, 2)
            for s in range(SLOTS):
                mm = nc.tensor.matmul(bank[BANK_PV][:, s:s + 1], bqk_row[0:1, s, :], one[0:1, 0:1], start=True, stop=True)
            mm.then_inc(bias_tp, 1)
            pe.wait_ge(lt_read, 4)
            for g in range(3):
                for c in range(NC):
                    if g:
                        pe.wait_ge(p_read, NC * (g - 1) + c + 1)
                    pe_p(pe, g, c)
            for u, x_bank in enumerate((BANK_X, BANK_G, BANK_U, BANK_X)):
                if u in (1, 2):
                    pe.wait_ge(p_read, 2 * NC + u)
                if u == 3:
                    pe.wait_ge(v_read, 2)
                pe_v(pe, u, bank[x_bank])
            pe.wait_ge(setup_ev, 8)
            pe.wait_ge(wd_ev, 4)
            pe.wait_ge(credit, 5)
            pe.wait_ge(q0_in[0], 16 * TERMS)
            pe.wait_ge(k0_in[0], 16 * TERMS)
            pe.wait_ge(qk1_in[0], 16 * 2 * TERMS)
            for m in range(NMX):
                pe_mx(pe, 0, m, 0)
            pe.wait_ge(v_read, NJ)
            pe_ct(pe, 0)
            with pe.Fori(0, B - 1) as b:
                pe_batch(pe, Turn(pe, b), False)
            pe_batch(pe, B - 1, True)

        def dve_stats(dve, b, t):
            if t == 0:
                dve.wait_ge(x_in, count(16 * (b + 1)))
            nc.vector.bn_stats(stats[:, t, :], xin[:, t, :]).then_inc(ln_step, 1)

        def dve_rsqrt(dve, b):
            n = LN_STEPS * b + NJ
            dve.wait_ge(ln_step, count(n))
            dve.sem_inc(held_dve, 1)
            for t in range(NJ):
                op = nc.vector.bn_aggr(mv[:, t, :], stats[:, t, :])
            op.then_inc(ln_step, 1)
            dve.wait_ge(ln_step, count(n + 1))
            var, guess, r, tmp = (nv[:, i, :] for i in range(4))
            nc.vector.tensor_scalar(var, mv[:, :, 1], EPS, None, ALU.add).then_inc(ln_step, 1)
            dve.wait_ge(ln_step, count(n + 2))
            nc.vector.tensor_scalar(guess.bitcast(I32), var.bitcast(I32), 1, None, ALU.logical_shift_right).then_inc(ln_step, 1)
            dve.wait_ge(ln_step, count(n + 3))
            n = n + 3
            nc.vector.tensor_scalar(r.bitcast(I32), guess.bitcast(I32), -1.0, float(RSQRT_GUESS), ALU.mult, ALU.add).then_inc(ln_step, 1)
            for _ in range(NEWTON):
                dve.wait_ge(ln_step, count(n + 1))
                nc.vector.tensor_tensor(tmp, r, r, ALU.mult).then_inc(ln_step, 1)
                dve.wait_ge(ln_step, count(n + 2))
                nc.vector.scalar_tensor_tensor(out=tmp, in0=tmp, scalar=-0.5, in1=var, op0=ALU.mult, op1=ALU.mult).then_inc(ln_step, 1)
                dve.wait_ge(ln_step, count(n + 3))
                nc.vector.scalar_tensor_tensor(out=r, in0=tmp, scalar=1.5, in1=r, op0=ALU.add, op1=ALU.mult).then_inc(ln_step, 1)
                n = n + 3

        def dve_rows(dve, b, t):
            if t == 0:
                dve.wait_ge(ln_step, count(LN_STEPS * (b + 1)))
            nc.vector.tensor_scalar(xn[:, t, :], xin[:, t, :], mv[:, t, 0:1], nv[:, 2, t:t + 1],
                                    ALU.subtract, ALU.mult).then_inc(xn_done, 1)

        def dve_high(dve, g, c):
            dve.wait_ge(p_read, count(NC * g + c + 1))
            if c == 0:
                dve.wait_ge(qks_out, count(16 * g))
            nc.vector.tensor_copy(qks[:, 0, c * CH:(c + 1) * CH], qf[:, c, :]).then_inc(hi_done, 1)

        def dve_mid(dve, g, c):
            dve.wait_ge(rest_done, count(NC * g + c + 1))
            nc.vector.tensor_copy(qks[:, 1, c * CH:(c + 1) * CH], qf[:, c, :]).then_inc(mid_done, 1)

        def dve_low(dve, g, c):
            dve.wait_ge(mid_done, count(NC * g + c + 1))
            nc.vector.tensor_tensor(qks[:, 2, c * CH:(c + 1) * CH], qf[:, c, :], qks[:, 1, c * CH:(c + 1) * CH],
                                    ALU.subtract).then_inc(split_done, 1)

        def dve_v(dve, b, u, x_bank):
            dve.wait_ge(v_done, count(4 * b + u + 1))
            for i in range(2):
                t = 2 * u + i
                nc.vector.tensor_tensor(vaug[:, t, :, 0:D], bank[x_bank][:, i * E:(i + 1) * E].rearrange("p (h d) -> p h d", h=H),
                                        bv[:, :].rearrange("p (h d) -> p h d", h=H), ALU.add).then_inc(v_read, 1)

        def dve_mx(dve, g, m):
            c, i, h = MX_TILES[m]
            n = min((i + 1) * P - c * CH, CH)
            src = bank[BANK_MX + m % 2][:, 0:n]
            dst = mx[:, h, i:i + 1]
            dve.wait_ge(mx_done, count(NMX * g + m + 1))
            if i * P < (c + 1) * CH:
                dve.wait_ge(mx_read, count(NMX * g + m + 1))
                if c:
                    dve.wait_ge(mx_read, count(MXR0 + NMX * g + (i * GH + h) + 1))
                dve.sem_inc(held_dve, 1)
                nc.vector.tensor_tensor_reduce(junk[:, m % 2, 0:n], src, causal[:, CH - n:CH], 1.0, dst if c else LOWEST,
                                               ALU.add, ALU.max, dst).then_inc(mx_read, 1)
            else:
                nc.vector.tensor_reduce(dst, src, AX.X, ALU.max).then_inc(mx_read, 1)

        def dve_cs(dve, g):
            dve.wait_ge(mx_read, count(MXR0 + NMX * (g + 1)))
            dve.wait_ge(ct_done, count(g))
            flat = mx[:, :, :].rearrange("p h i -> p (h i)")
            nc.vector.tensor_scalar(cs[:, 0, :], flat, -1.0, None, ALU.mult).then_inc(cs_step, 1)
            dve.wait_ge(cs_step, count(g + 1))
            nc.vector.scalar_tensor_tensor(out=cs[:, 1, :], in0=flat, scalar=-1.0, in1=cs[:, 0, :],
                                           op0=ALU.mult, op1=ALU.subtract).then_inc(cs_done, 1)

        def dve_turn(dve, w):
            dve.wait_ge(o_read, count(O0 + w + 1))
            dve.wait_ge(on_done, count(w + FREE))
            dve.sem_inc(held_dve, 1)
            nc.vector.transpose(o_rows[:, :, :].rearrange("p n c -> p (n c)"), osb[:, :]).then_inc(o_turned, 1)
            dve.wait_ge(o_turned, count(w + 1 + FREE))
            nc.vector.reciprocal(rsum[:, :], o_rows[:, :, D]).then_inc(rsum_done, 1)

        def dve_pair(dve, b, s, c):
            dve.wait_ge(on_done, count(NC * (SLOTS * b + s) + c + 1 + FREE))
            dve.wait_ge(pj_done, count(4 * b + FREE))
            dve.sem_inc(held_dve, 1)
            nc.vector.transpose(oT[:, s // 2, c * CH:(c + 1) * CH], pair[:, c, :, :].rearrange("p n c -> p (n c)")).then_inc(pair_done, 1)

        def dve_gate(dve, b, c, m):
            dve.wait_ge(tg_done, count(4 * b + KT * c + m + 1))
            nc.vector.scalar_tensor_tensor(out=acc(c, m), in0=tg[:, m, :], scalar=1.0, in1=acc(c, m),
                                           op0=ALU.add, op1=ALU.mult).then_inc(gate_done, 1)

        SPLIT_AT = ((0, 0, 0, 0), (0, 0, 2, 1), (1, 1, 0, 0), (2, 2, 0, 0), (1, 2, 2, 1), (2, 3, 0, 1))

        def dve_batch(dve, b, last):
            for s in range(SLOTS):
                g = SLOTS * b + s
                for k in range(NSTEP):
                    for h in range(GH):
                        i = GH * k + h
                        if not (last and s == SLOTS - 1):
                            dve_mx(dve, g + 1, i)
                        unit = k // 3
                        t = UNITS * (s % 2) + unit
                        if k % 3 == 1 and h == 3:
                            dve.wait_ge(th_done, count(UNITS * g + unit + 1))
                            dve.wait_ge(h_done, count(UNITS * g + unit + FREE))
                            nc.vector.scalar_tensor_tensor(out=gated[:, :], in0=th[:, :], scalar=1.0, in1=bank[BANK_G][:, :],
                                                           op0=ALU.add, op1=ALU.mult).then_inc(g_read, 1)
                        if k % 3 == 2 and h == 3:
                            dve.wait_ge(u_done, count(UNITS * g + unit + 1 + FREE))
                            dve.wait_ge(g_read, count(UNITS * g + unit + 1 + FREE))
                            if unit == 0:
                                dve.wait_ge(dn_done, count(KT * g + FREE))
                            nc.vector.scalar_tensor_tensor(out=hid[:, unit, :], in0=bank[BANK_U][:, :], scalar=gus[:, t:t + 1],
                                                           in1=gated[:, :], op0=ALU.mult, op1=ALU.mult).then_inc(h_done, 1)
                        for part, k_at, h_at, piece in SPLIT_AT:
                            if (k, h) == (k_at, h_at) and not (last and s >= SLOTS - 2):
                                (dve_high, dve_mid, dve_low)[part](dve, g + 2, piece)
                        if s and (k, h) == (1, 2):
                            dve_turn(dve, NC * g - 1)
                        if s == 2 and (k, h) == (5, 1):
                            dve_pair(dve, b, s - 1, 1)
                        if (k, h) == (7, 0):
                            dve_turn(dve, NC * g)
                        if s % 2 and (k, h) == (10, 1):
                            dve_pair(dve, b, s, 0)
                        if s == 2 and k == 4 and h % 2:
                            dve_gate(dve, b, 0, h // 2)
                        if s == 0 and not last and h == 1 and 2 <= k < 2 + NJ:
                            dve_stats(dve, b + 1, k - 2)
                        if s == 1 and not last and k < 4 and h % 2:
                            if k == 0 and h == 1:
                                dve.wait_ge(lt_done, count(4 * (b + 1)))
                                dve.wait_ge(y_done, count(4 * b + FREE))
                            dve_rows(dve, b + 1, 2 * k + h // 2)
                if s == 0 and not last:
                    dve_rsqrt(dve, b + 1)
                if not (last and s == SLOTS - 1):
                    dve_cs(dve, g + 1)
                for m in range(KT):
                    dve.wait_ge(dn_done, count(KT * g + m + 1 + FREE))
                    if s % 2 == 0:
                        dve.wait_ge(zg_done, count(4 * b + FREE))
                        nc.vector.tensor_copy(acc(s // 2, m), bank[BANK_G + m][:, :]).then_inc(dn_read, 1)
                    else:
                        dve.wait_ge(dn_read, count(KT * g))
                        nc.vector.tensor_tensor(acc(s // 2, m), bank[BANK_G + m][:, :], acc(s // 2, m), ALU.add).then_inc(dn_read, 1)
            dve_turn(dve, NC * SLOTS * (b + 1) - 1)
            for m in range(KT):
                dve_gate(dve, b, 1, m)
            dve_pair(dve, b, SLOTS - 1, 1)
            if not last:
                dve.wait_ge(pv_done, count(PV0 + NSTEP * SLOTS * (b + 1)))
                for u, x_bank in enumerate((BANK_X, BANK_G, BANK_U, BANK_X)):
                    dve_v(dve, b + 1, u, x_bank)
            for u, x_bank in enumerate((BANK_G, BANK_U, BANK_X, BANK_G)):
                rows = z[:, 2 * u:2 * u + 2, :].rearrange("p i e -> p (i e)")
                dve.wait_ge(pj_done, count(4 * b + u + 1 + FREE))
                dve.wait_ge(lt_done, count(4 * (b + 1 if last else b + 2)))
                nc.vector.tensor_tensor(z[:, 2 * u:2 * u + 2, :], bank[x_bank][:, :].rearrange("p (i e) -> p i e", i=2),
                                        bp[:, :].rearrange("p (o e) -> p o e", o=1).broadcast_to([P, 2, E]), ALU.add).then_inc(z_done, 1)
                dve.wait_ge(z_done, count(4 * b + u + 1 + FREE))
                dve.wait_ge(gate_done, count(4 * b + u + 1 + FREE))
                nc.vector.tensor_tensor(rows, rows, acc(u // 2, u % 2), ALU.mult).then_inc(zg_done, 1)

        @block.vector
        def _(dve):
            for par in range(2):
                nc.vector.memset(ks[par][KROWS:KROWS + CPARTS, :, :], 1.0).then_inc(consts, 1)
            nc.vector.memset(vaug[:, :, :, :], float(E) ** 0.5).then_inc(consts, 1)
            nc.vector.memset(junk[:, 0, 0:2], 0.0).then_inc(exp_done, EXP0)
            nc.vector.memset(junk[:, 0, 2:4], 0.0).then_inc(mx_read, MXR0)
            nc.vector.memset(junk[:, 0, 4:6], 0.0).then_inc(pv_done, PV0)
            nc.vector.memset(junk[:, 0, 6:8], 0.0).then_inc(o_read, O0)
            nc.vector.memset(junk[:, 0, 8:10], 0.0).then_inc(pair_done, PAIR0)
            for i, done in enumerate((pj_done, z_done, gate_done, dn_done, h_done, zg_done, y_done, on_done, g_read, u_done, out_done, o_turned)):
                nc.vector.memset(junk[:, 1, 2 * i:2 * i + 2], 0.0).then_inc(done, FREE)
            nc.vector.memset(junk[:, 0, 10:12], 0.0).then_inc(credit, 5)
            for t in range(NJ):
                dve_stats(dve, 0, t)
            dve_rsqrt(dve, 0)
            for t in range(NJ):
                dve_rows(dve, 0, t)
            dve.wait_ge(w_in, count(16 * N_W_IN_ALL))
            for w in (gi, ui, di):
                nc.vector.tensor_scalar(w.bitcast(F32), w, -ZERO_POINT, None, ALU.add).then_inc(w_conv, 1)
            n = 0
            for src, r, rows in ((wa[:, 0, :], 0, P), (wa[:, 1, :], 1, P), (ba, 2, 1)):
                direct, cross = rtmp[r][0:rows, :], rtmp2[r][0:rows, :]
                even, odd = (src.rearrange("p (n two) -> p n two", two=2)[:, :, i] for i in range(2))
                s_even, s_odd = (sinr[0:rows, :].rearrange("p (n two) -> p n two", two=2)[:, :, i] for i in range(2))
                c_even, c_odd = (cross.rearrange("p (n two) -> p n two", two=2)[:, :, i] for i in range(2))
                nc.vector.tensor_tensor(direct, src, cosr[0:rows, :], ALU.mult).then_inc(rope_step, 1)
                nc.vector.tensor_tensor(c_even, odd, s_even, ALU.mult).then_inc(rope_step, 1)
                nc.vector.tensor_tensor(c_odd, even, s_odd, ALU.mult).then_inc(rope_step, 1)
                n += 3
                dve.wait_ge(rope_step, count(n))
                for side in range(2):
                    dst = wqk[:, r, :, side * 64:(side + 1) * 64] if r < KT else bqk_row[:, :, side * 64:(side + 1) * 64]
                    op = nc.vector.tensor_tensor(dst, direct[:, side * E:(side + 1) * E].rearrange("p (s n) -> p s n", s=SLOTS),
                                                 cross[:, side * E:(side + 1) * E].rearrange("p (s n) -> p s n", s=SLOTS), ALU.add)
                if r:
                    op.then_inc(rope_done, 1)
            nc.vector.tensor_scalar(gsh[:, :], gsc[:, :], 0.5, None, ALU.mult).then_inc(rope_step, 1)
            dve.wait_ge(rope_step, n + 1)
            nc.vector.tensor_tensor(gus[:, :], gsh[:, :], usc[:, :], ALU.mult).then_inc(rope_step, 1)
            for g in range(2):
                for part in (dve_high, dve_mid, dve_low):
                    for c in range(NC):
                        part(dve, g, c)
            for u in range(4):
                dve.wait_ge(setup_tp, 8 + u + 1)
                nc.vector.scalar_tensor_tensor(out=wd[:, 2 * u:2 * u + 2, :], in0=bank[u][:, :].rearrange("p (i e) -> p i e", i=2),
                                               scalar=0.5, in1=dsc[:, :].rearrange("p (o e) -> p o e", o=1).broadcast_to([P, 2, E]),
                                               op0=ALU.mult, op1=ALU.mult).then_inc(wd_ev, 1)
            dve.wait_ge(consts, N_CONSTS)
            for u, x_bank in enumerate((BANK_X, BANK_G, BANK_U, BANK_X)):
                dve_v(dve, 0, u, x_bank)
            for m in range(NMX):
                dve_mx(dve, 0, m)
            dve_cs(dve, 0)
            with dve.Fori(0, B - 1) as b:
                dve_batch(dve, Turn(dve, b), False)
            dve_batch(dve, B - 1, True)


N_W_IN_ALL = 6 + 2 * GH + 4 + 3

_INS = ['L0_attn_x', 'L0_attn_w_attn', 'L0_attn_b_attn', 'L0_attn_w_proj', 'L0_attn_b_proj', 'L0_ffn_gate_w',
        'L0_ffn_gate_scale', 'L0_ffn_up_w', 'L0_ffn_up_scale', 'L0_ffn_down_w', 'L0_ffn_down_scale']


def _rope_rows():
    import numpy as np

    freqs = np.float32(10000.0) ** (-(np.arange(0, D, 2, dtype=np.float32) / np.float32(D)))
    angle = np.outer(np.arange(H, dtype=np.float32), freqs.astype(np.float32)).astype(np.float32)
    cos, sin = np.cos(angle).astype(np.float32), np.sin(angle).astype(np.float32)
    cos = np.stack([cos, cos], -1).reshape(1, E)
    sin = np.stack([-sin, sin], -1).reshape(1, E)
    return np.concatenate([cos, cos], 1), np.concatenate([sin, sin], 1)


def kernel(**inputs):
    import numpy as _np
    import concourse.bacc as _bacc
    from concourse import mybir as _mybir
    from concourse.bass_utils import run_bass_kernel_spmd as _run

    nc = _bacc.Bacc("TRN2", target_bir_lowering=False, num_devices=1)
    arrays, args = {}, []
    rope_cos, rope_sin = _rope_rows()
    named = [(name, inputs[name]) for name in _INS] + [("rope_cos", rope_cos), ("rope_sin", rope_sin)]
    for name, a in named:
        a = _np.ascontiguousarray(a)
        arrays[f"in_{name}"] = a
        args.append(nc.dram_tensor(f"in_{name}", a.shape, _mybir.dt.from_np(a.dtype), kind="ExternalInput").ap())
    args.append(nc.dram_tensor("out_y", (B, T, E), F32, kind="ExternalOutput").ap())
    build(nc, *args)
    r = _run(nc, [arrays], core_ids=[0])
    return r.results[0]["out_y"]
```

```python
from contextlib import ExitStack

import concourse.bass as bass
from concourse import mybir
from concourse.alu_op_type import AluOpType as ALU

ACT = mybir.ActivationFunctionType
AX = mybir.AxisListType
F32 = mybir.dt.float32
F32R = mybir.dt.float32r
BF16 = mybir.dt.bfloat16
I32 = mybir.dt.int32

P = 128
B, T, E = 4, 1024, 256
H, D = 16, 16
I = 1024
KT = E // P
GH = 4
SLOTS = H // GH
CH = 512
NC = T // CH
NJ = T // P
STEPS = [(c, j) for c in range(NC) for j in range((c + 1) * CH // P)]
NSTEP = len(STEPS)
NPOS = NSTEP * GH
MX_TILES = [(c, i, h) for c, tiles in ((0, (2, 3, 1, 0, 4, 5, 6, 7)), (1, (7, 6, 5, 4))) for i in tiles for h in range(GH)]
NMX = len(MX_TILES)
KEEP_STEPS = (3, 4, 6, 7)
LT_UNITS = [(half, k) for half in (1, 0) for k in range(KT)]
LT_STEPS = (8, 10)
BLK = 32
NBLK = CH // BLK
PAIRS = SLOTS // 2
TERMS = 6
KROWS = TERMS * D
PARTS = 3
CPARTS = 2
UNITS = 4
SPLIT_TERMS = ((0, 0), (0, 1), (1, 0))
GATED = 2 * KT * len(SPLIT_TERMS)
GATED_AT = [[i] for i in range(3)] + [[3, 4], [5, 6]] + [[i + 2] for i in range(5, NPOS - 2)] + [[], []]
assert sum(GATED_AT, []) == list(range(UNITS * GATED))
PR = 2
LOWEST = -3.0e38
NEWTON = 3
STATS_AT = range(13, 13 + 3 * NJ, 3)
assert len(STATS_AT) == NJ
RSQRT_STEPS = 4 + 3 * NEWTON
LN_STEPS = NJ + RSQRT_STEPS
EPS = 1e-5
ZERO_POINT = 128.0
RSQRT_GUESS = 0x5F3759DF
CHUNKS_AT = ((0, 1), (1, 0), (0, 1), (0, 1))
BANK_ST, BANK_MX, BANK_PV, BANK_G, BANK_U, BANK_X = 0, 2, 4, 5, 6, 7
LT_BANKS = (BANK_X, BANK_G, BANK_U, BANK_ST)


def diagonal(k):
    c, j = STEPS[k]
    return j * P >= c * CH


def step_tokens(k):
    c, j = STEPS[k]
    first = max(c * CH, j * P)
    return first, (c + 1) * CH - first


assert NMX == NPOS


class Turn:

    def __init__(self, engine, turn, per=1, more=0, products=None):
        self.engine, self.turn, self.per, self.more = engine, turn, per, more
        self.products = {1: turn} if products is None else products

    def __add__(self, n):
        return Turn(self.engine, self.turn, self.per, self.more + n, self.products)

    def __sub__(self, n):
        return self + -n

    def __mul__(self, n):
        return Turn(self.engine, self.turn, self.per * n, self.more * n, self.products)

    __radd__, __rmul__ = __add__, __mul__


def count(n):
    if not isinstance(n, Turn):
        return n
    if n.per not in n.products:
        n.products[n.per] = n.engine.snap(n.turn * n.per)
    product = n.products[n.per]
    return product + n.more if n.more else product


def build(nc, x, w_attn, b_attn, w_proj, b_proj, gate_w, gate_scale, up_w, up_scale, down_w, down_scale,
          rope_cos, rope_sin, out):
    nc.disable_value_cache = True
    ctx = ExitStack()
    with ctx:
        def sb(name, shape, dt=F32):
            return ctx.enter_context(nc.sbuf_tensor(name, shape, dt))

        def sem(name):
            return ctx.enter_context(nc.semaphore(name))

        ident = sb("ident", [P, P])
        identb = sb("identb", [P, P], BF16)
        one = sb("one", [1, 2])
        causal = sb("causal", [P, CH], BF16)
        wv = sb("wv", [P, 2, KT, E], F32R)
        wqk = sb("wqk", [P, 2, KT, SLOTS, P], F32R)
        bqk = sb("bqk", [P, SLOTS])
        bv = sb("bv", [P, E])
        wp = sb("wp", [P, PAIRS, E])
        bp = sb("bp", [P, E])
        wg = sb("wg", [P, 2, KT, I], F32R)
        wu = sb("wu", [P, 2, KT, I], F32R)
        wd = sb("wd", [P, 2, I // P, E], F32R)
        gsc = sb("gsc", [P, I // P])
        usc = sb("usc", [P, I // P])
        gsh = sb("gsh", [P, I // P])
        gus = sb("gus", [P, I // P])
        xin = sb("xin", [P, NJ, E])
        stats = sb("stats", [P, NJ, 6])
        mv = sb("mv", [P, NJ, 2])
        nv = sb("nv", [P, 4, NJ])
        xnT = sb("xnT", [P, 2, KT, T], F32R)
        xnF = sb("xnF", [P, 2, KT, CH], F32R)
        qf = sb("qf", [P, NC, CH])
        qks = sb("qks", [P, PARTS, T], BF16)
        qs = [sb(f"qs{i}", [KROWS + CPARTS, GH, T], BF16) for i in range(2)]
        ks = [sb(f"ks{i}", [KROWS + CPARTS, GH, T], BF16) for i in range(2)]
        VSTEP = 2 * D + 1
        vals_all = sb("vals", [P, NJ * PAIRS * GH * VSTEP + BLK - D - 1])
        vals = vals_all[:, 0:NJ * PAIRS * GH * VSTEP].rearrange("p (j t q d) -> p j t q d", j=NJ, t=PAIRS, q=GH)
        nothing = sb("nothing", [P, 19])
        mx = sb("mx", [P, GH, NJ])
        cs = sb("cs", [P, CPARTS, GH * NJ], BF16)
        ct = sb("ct", [CPARTS * GH * NJ, P], BF16)
        prob = sb("prob", [P, PR, GH, CH])
        quant = [prob[:, i, :, :].rearrange("p h c -> p (h c)").bitcast(I32) for i in range(2)]
        gi, ui = (quant[i].rearrange("p (n h) -> p n h", h=E) for i in range(2))
        wd_full = prob[:, 0, :, :]
        th = sb("th", [P, CH])
        gated = sb("gated", [P, CH])
        hid = sb("hid", [P, 2, UNITS, CH], F32R)
        gacc = sb("gacc", [P, NJ, E])
        flat_g = gacc[:, :, :].rearrange("p k t -> p (k t)")
        di = flat_g.bitcast(I32).rearrange("p (k i) -> p k i", i=I)
        wa = flat_g[:, 0:4 * E].rearrange("p (k n) -> p k n", k=KT)
        ba = flat_g[0:1, 4 * E:6 * E]
        bqk_row = flat_g[0:1, 6 * E:8 * E].rearrange("o (s n) -> o s n", s=SLOTS)
        o_rows = sb("o_rows", [P, NBLK, BLK])
        rsum = sb("rsum", [P, NBLK])
        pair = sb("pair", [P, NC, NBLK, BLK])
        oT = sb("oT", [P, PAIRS, T])
        flat_v = vals_all
        flat_o = oT[:, :, :].rearrange("p s t -> p (s t)")
        cosr, sinr = flat_v[:, 0:2 * E], flat_v[:, 2 * E:4 * E]
        rtmp = [flat_v[:, 4 * E:6 * E], flat_v[:, 6 * E:8 * E], flat_o[:, 6 * E:8 * E]]
        rtmp2 = [flat_o[:, 2 * r * E:2 * (r + 1) * E] for r in range(3)]
        dsc = o_rows[:, 0:E // BLK, :].rearrange("p n c -> p (n c)")
        wv_full = pair[:, 0, :, :].rearrange("p n c -> p (n c)").rearrange("p (k n) -> p k n", k=KT)
        z = (gated, th)
        bank = [ctx.enter_context(nc.psum_tensor(f"bank{i}", [P, CH], F32)) for i in range(8)]
        scratch = nc.dram_tensor("qk_parts", (2, P, PARTS, T), BF16, kind="Internal").ap()

        w_in = sem("w_in")
        rope_in = sem("rope_in")
        quant_in = sem("quant_in")
        consts = sem("consts")
        pool_step = sem("pool_step")
        credit = sem("credit")
        w_conv = sem("w_conv")
        rope_products = sem("rope_products")
        rope_step = sem("rope_step")
        rope_done = sem("rope_done")
        setup_tp = sem("setup_tp")
        setup_ev = sem("setup_ev")
        setup_low = sem("setup_low")
        down_in = sem("down_in")
        ones_done = sem("ones_done")
        wd_scaled = sem("wd_scaled")
        wd_high = sem("wd_high")
        wd_low = sem("wd_low")
        bias_tp = sem("bias_tp")
        bias_ev = sem("bias_ev")
        x_in = sem("x_in")
        xres_in = sem("xres_in")
        ln_step = sem("ln_step")
        xn_done = sem("xn_done")
        lt_done = sem("lt_done")
        lt_read = sem("lt_read")
        lt_high = sem("lt_high")
        xf_done = sem("xf_done")
        wv_high = sem("wv_high")
        wv_low = sem("wv_low")
        p_done = sem("p_done")
        p_read = sem("p_read")
        hi_done = sem("hi_done")
        rest_done = sem("rest_done")
        mid_done = sem("mid_done")
        split_done = sem("split_done")
        qks_out = sem("qks_out")
        q0_in, k0_in, qk1_in = ([sem(f"{n}_in{i}") for i in range(2)] for n in ("q0", "k0", "qk1"))
        v_done = sem("v_done")
        v_read = sem("v_read")
        mx_done = sem("mx_done")
        mx_read = sem("mx_read")
        cs_step = sem("cs_step")
        cs_done = sem("cs_done")
        ct_done = sem("ct_done")
        ct_read = sem("ct_read")
        ct_in = sem("ct_in")
        st_done = sem("st_done")
        exp_done = sem("exp_done")
        mask_done = sem("mask_done")
        pv_done = sem("pv_done")
        o_read = sem("o_read")
        rsum_done = sem("rsum_done")
        on_done = sem("on_done")
        pair_done = sem("pair_done")
        g_done = sem("g_done")
        th_done = sem("th_done")
        g_read = sem("g_read")
        u_done = sem("u_done")
        h_done = sem("h_done")
        hid_high_done = sem("hid_high_done")
        hid_low_done = sem("hid_low_done")
        dn_done = sem("dn_done")
        dn_read = sem("dn_read")
        tg_done = sem("tg_done")
        gate_done = sem("gate_done")
        pj_done = sem("pj_done")
        z_done = sem("z_done")
        zg_done = sem("zg_done")
        y_done = sem("y_done")
        out_done = sem("out_done")
        held_dve, held_pe, held_pool, held_sp = (sem(f"held_{e}") for e in ("dve", "pe", "pool", "sp"))

        EXP0, MXR0, PV0, O0, PAIR0 = 2, 2, PR, 1, NC
        FREE = 1
        block = ctx.enter_context(nc.Block())

        def load_x(sp, b):
            sp.dma_start(xin[:, :, :], x[bass.ds(count(b), 1), :, :].rearrange("o (i p) e -> p (o i) e", p=P)).then_inc(x_in, 16)

        def store_parts(sp, g, par):
            sp.wait_ge(split_done, count(NC * (g + 1)))
            sp.dma_start(scratch[par], qks[:, :, :]).then_inc(qks_out, 16)
            sp.wait_ge(qks_out, count(16 * (g + 1)))

        def load_half(sp, par, side, c, done):
            dst = (qs, ks)[side][par]
            parts = scratch[par, side * GH * D:(side + 1) * GH * D].rearrange("(h d) a t -> a d h t", h=GH)
            for row, part in enumerate(((0, 0, 0, 1, 1, 2), (0, 1, 2, 0, 1, 0))[side]):
                sp.dma_start(dst[row * D:(row + 1) * D, :, c * CH:(c + 1) * CH],
                             parts[part, :, :, c * CH:(c + 1) * CH]).then_inc(done[par], 16)

        def load_shift(sp, g, par):
            sp.wait_ge(ct_read, count(g + 1))
            for a in range(CPARTS):
                sp.dma_start(qs[par][KROWS + a:KROWS + a + 1, :, :].rearrange("o h (i c) -> o (h i) c", c=P),
                             ct[a * GH * NJ:(a + 1) * GH * NJ, :]).then_inc(ct_in, 16)

        def sp_batch(sp, b, last):
            if not last:
                sp.wait_ge(lt_done, count(4 * (b + 1)))
                sp.sem_inc(held_sp, 1)
                sp.wait_ge(out_done, count(16 * 4 * b + FREE))
                sp.sem_inc(held_sp, 1)
                load_x(sp, b + 1)
            for s in range(SLOTS):
                g = SLOTS * b + s
                par = s % 2
                if s == 2:
                    if not last:
                        sp.wait_ge(lt_done, count(4 * (b + 2)))
                    else:
                        sp.wait_ge(out_done, count(16 * 4 * b + FREE))
                    sp.sem_inc(held_sp, 1)
                    sp.dma_start(xin[:, :, :], x[bass.ds(count(b), 1), :, :].rearrange("o (i p) e -> p (o i) e", p=P)).then_inc(xres_in, 16)
                more = not (last and s >= SLOTS - 2)
                if more:
                    store_parts(sp, g + 2, par)
                    sp.wait_ge(st_done, count(NPOS * g + GH * 4))
                    load_half(sp, par, 0, 0, q0_in)
                    sp.wait_ge(st_done, count(NPOS * g + GH * 8))
                    load_half(sp, par, 1, 0, k0_in)
                if not (last and s == SLOTS - 1):
                    load_shift(sp, g + 1, 1 - par)
                if more:
                    sp.wait_ge(st_done, count(NPOS * (g + 1)))
                    load_half(sp, par, 0, 1, qk1_in)
                    load_half(sp, par, 1, 1, qk1_in)
            for u in range(4):
                sp.wait_ge(y_done, count(4 * b + u + 1 + FREE))
                sp.sem_inc(held_sp, 1)
                sp.dma_start(out[bass.ds(count(b), 1), 2 * u * P:2 * (u + 1) * P, :].rearrange("o (i p) e -> p (o i) e", p=P),
                             xin[:, 2 * u:2 * u + 2, :]).then_inc(out_done, 16)

        @block.sync
        def _(sp):
            load_x(sp, 0)
            sp.dma_start(wa, w_attn[:, 0:2 * E].rearrange("(k p) n -> p k n", p=P)).then_inc(rope_in, 16)
            sp.dma_start(ba, b_attn[0:2 * E].rearrange("(o n) -> o n", o=1)).then_inc(rope_in, 16)
            sp.dma_start(cosr, rope_cos.broadcast_to([P, 2 * E])).then_inc(rope_in, 16)
            sp.dma_start(sinr, rope_sin.broadcast_to([P, 2 * E])).then_inc(rope_in, 16)
            sp.dma_start(wv_full, w_attn[:, 2 * E:3 * E].rearrange("(k p) n -> p k n", p=P)).then_inc(w_in, 16)
            sp.dma_start(bv[:, :], b_attn[2 * E:3 * E].rearrange("(o n) -> o n", o=1).broadcast_to([P, E])).then_inc(w_in, 16)
            for q in range(GH):
                for half in range(2):
                    sp.dma_start(wp[BLK * q + D * half:BLK * q + D * (half + 1), :, :],
                                 w_proj.rearrange("(t s q d) n -> q s d t n", t=PAIRS, s=2, q=GH)[q, half]).then_inc(w_in, 16)
            sp.dma_start(bp[:, :], b_proj.rearrange("(o n) -> o n", o=1).broadcast_to([P, E])).then_inc(w_in, 16)
            sp.dma_start(gsc[:, :], gate_scale.rearrange("(n p) -> p n", p=P), allow_slow_non_contiguous=True).then_inc(w_in, 16)
            sp.dma_start(usc[:, :], up_scale.rearrange("(n p) -> p n", p=P), allow_slow_non_contiguous=True).then_inc(w_in, 16)
            sp.dma_start(dsc, down_scale.rearrange("(o n) -> o n", o=1).broadcast_to([P, E])).then_inc(w_in, 16)
            for w, src in ((gi, gate_w), (ui, up_w)):
                sp.dma_start(w, src.rearrange("(n p) h -> p n h", p=P)).then_inc(quant_in, 16)
            sp.wait_ge(rope_done, 2)
            sp.wait_ge(bias_tp, 1)
            sp.dma_start(di, down_w.rearrange("(n p) h -> p n h", p=P)).then_inc(down_in, 16)
            for g in range(2):
                store_parts(sp, g, g)
                load_half(sp, g, 0, 0, q0_in)
                load_half(sp, g, 1, 0, k0_in)
                load_half(sp, g, 0, 1, qk1_in)
                load_half(sp, g, 1, 1, qk1_in)
            load_shift(sp, 0, 0)
            with sp.Fori(0, B - 1) as b:
                sp_batch(sp, Turn(sp, b), False)
            sp_batch(sp, B - 1, True)
            sp.wait_ge(out_done, count(16 * 4 * B + FREE))

        def pool_rest(pool, g, c):
            pool.wait_ge(hi_done, count(NC * g + c + 1))
            nc.gpsimd.tensor_tensor(qf[:, c, :], qf[:, c, :], qks[:, 0, c * CH:(c + 1) * CH], ALU.subtract).then_inc(rest_done, 1)

        def pool_hid(pool, g, unit):
            pool.wait_ge(hid_high_done, count(UNITS * g + unit + 1))
            nc.gpsimd.tensor_tensor(hid[:, 1, unit, :], gated[:, :], hid[:, 0, unit, :].bitcast(F32), ALU.subtract).then_inc(hid_low_done, 1)

        def pool_low(pool, g, c):
            pool.wait_ge(mid_done, count(NC * g + c + 1))
            nc.gpsimd.tensor_tensor(qks[:, 2, c * CH:(c + 1) * CH], qf[:, c, :], qks[:, 1, c * CH:(c + 1) * CH],
                                    ALU.subtract).then_inc(split_done, 1)

        def pool_row(pool, b, t):
            if t == 0:
                pool.wait_ge(ln_step, count(LN_STEPS * (b + 1)))
                pool.sem_inc(held_pool, 1)
            nc.gpsimd.tensor_scalar(xin[:, t, :], xin[:, t, :], mv[:, t, 0:1], nv[:, 2, t:t + 1],
                                    ALU.subtract, ALU.mult).then_inc(xn_done, 1)

        def pool_norm(pool, b, s, c):
            w = NC * (SLOTS * b + s) + c
            pool.wait_ge(rsum_done, count(w + 1))
            if s % 2 == 0:
                pool.wait_ge(pair_done, count(NC * PAIRS * b + NC * (s // 2) + c + 1))
            nc.gpsimd.tensor_tensor(pair[:, c, :, D * (s % 2):D * (s % 2 + 1)], o_rows[:, :, s % 2:s % 2 + D],
                                    rsum[:, :].rearrange("p (n o) -> p n o", o=1).broadcast_to([P, NBLK, D]), ALU.mult).then_inc(on_done, 1)

        def pool_y(pool, b, u):
            pool.wait_ge(zg_done, count(4 * b + u + 1 + FREE))
            pool.wait_ge(xres_in, count(16 * (b + 1)))
            nc.gpsimd.tensor_tensor(xin[:, 2 * u:2 * u + 2, :], gacc[:, 2 * u:2 * u + 2, :], xin[:, 2 * u:2 * u + 2, :], ALU.add).then_inc(y_done, 1)

        def pool_batch(pool, b, last):
            for s in range(SLOTS):
                g = SLOTS * b + s
                for k in range(NSTEP):
                    if diagonal(k):
                        pool.wait_ge(exp_done, count(EXP0 + NPOS * g + GH * (k + 1)))
                        pool.sem_inc(held_pool, 1)
                        own = prob[:, k % PR, :, 0:P]
                        nc.gpsimd.affine_select(out=own, in_=own, compare_op=ALU.is_ge, fill=0.0, base=0,
                                                pattern=[[0, GH], [1, P]], channel_multiplier=-1).then_inc(mask_done, 1)
                    if not (last and s >= SLOTS - 2):
                        if k < NC:
                            pool_rest(pool, g + 2, k)
                        if 4 <= k < 4 + NC:
                            pool_low(pool, g + 2, k - 4)
                    if s == 1 and not last and 4 <= k < 8:
                        for t in range(2 * k - 8, 2 * k - 6):
                            pool_row(pool, b + 1, t)
                    if k == 3 and s:
                        pool_norm(pool, b, s - 1, 1)
                    if k % 3 == 0 and k:
                        pool_hid(pool, g, k // 3 - 1)
                    if k == 8:
                        pool_norm(pool, b, s, 0)
                pool_hid(pool, g, UNITS - 1)
            pool_norm(pool, b, SLOTS - 1, 1)
            for u in range(4):
                pool_y(pool, b, u)

        N_CONSTS = 2
        ROPE_SOURCES = ((wa[:, 0, :], P), (wa[:, 1, :], P), (ba, 1))

        @block.gpsimd
        def _(pool):
            nc.gpsimd.memset(ident[:, :], 0.0).then_inc(pool_step, 1)
            nc.gpsimd.memset(causal[:, :], 0.0).then_inc(pool_step, 1)
            nc.gpsimd.memset(one[:, :], 1.0).then_inc(consts, 1)
            pool.wait_ge(pool_step, 2)
            nc.gpsimd.affine_select(out=ident[:, :], in_=ident[:, :], compare_op=ALU.not_equal, fill=1.0,
                                    base=0, pattern=[[-1, P]], channel_multiplier=1).then_inc(pool_step, 1)
            nc.gpsimd.affine_select(out=causal[:, CH - P:CH], in_=causal[:, CH - P:CH], compare_op=ALU.is_ge, fill=LOWEST,
                                    base=0, pattern=[[-1, P]], channel_multiplier=1).then_inc(consts, 1)
            pool.wait_ge(pool_step, 3)
            nc.gpsimd.tensor_copy(identb[:, :], ident[:, :]).then_inc(pool_step, 1)
            pool.wait_ge(rope_in, 16 * 4)
            pool.wait_ge(pool_step, 4)
            for r, (src, rows) in enumerate(ROPE_SOURCES):
                direct, cross = rtmp[r][0:rows, :], rtmp2[r][0:rows, :]
                even, odd = (src.rearrange("p (n two) -> p n two", two=2)[:, :, i] for i in range(2))
                s_even, s_odd = (sinr[0:rows, :].rearrange("p (n two) -> p n two", two=2)[:, :, i] for i in range(2))
                c_even, c_odd = (cross.rearrange("p (n two) -> p n two", two=2)[:, :, i] for i in range(2))
                nc.gpsimd.tensor_tensor(direct, src, cosr[0:rows, :], ALU.mult).then_inc(rope_products, 1)
                nc.gpsimd.tensor_tensor(c_even, odd, s_even, ALU.mult).then_inc(rope_products, 1)
                nc.gpsimd.tensor_tensor(c_odd, even, s_odd, ALU.mult).then_inc(rope_products, 1)
            pool.wait_ge(consts, N_CONSTS)
            pool.wait_ge(rope_products, 9)
            for par in range(2):
                pool.wait_ge(pool_step, 4 + par)
                nc.gpsimd.memset(ks[par][KROWS:KROWS + CPARTS, :, :], 1.0).then_inc(pool_step, 1)
            pool.wait_ge(pool_step, 6)
            pool.wait_ge(rope_done, 2)
            nc.gpsimd.memset(vals_all[:, :], float(E) ** 0.5).then_inc(ones_done, 1)
            pool.wait_ge(ones_done, 1)
            pool.wait_ge(wv_high, 1)
            nc.gpsimd.tensor_tensor(wv[:, 1, :, :], wv_full, wv[:, 0, :, :].bitcast(F32), ALU.subtract).then_inc(wv_low, 1)
            for g in range(2):
                for c in range(NC):
                    pool_rest(pool, g, c)
            for u in range(4):
                high, low = (wd[:, i, 2 * u:2 * u + 2, :] for i in range(2))
                pool.wait_ge(wd_high, u + 1)
                nc.gpsimd.tensor_tensor(low, wd_full[:, u, :].rearrange("p (i e) -> p i e", i=2), high.bitcast(F32), ALU.subtract).then_inc(wd_low, 1)
            with pool.Fori(0, B - 1) as b:
                pool_batch(pool, Turn(pool, b), False)
            pool_batch(pool, B - 1, True)


        def act_lt(act, b, u, x_bank):
            half, k = LT_UNITS[u]
            act.wait_ge(lt_done, count(4 * b + u + 1))
            nc.scalar.activation(xnT[:, 0, k, half * CH:(half + 1) * CH], bank[x_bank][:, :], ACT.Copy).then_inc(lt_high, 1)

        def act_p(act, g, s, n, c):
            act.wait_ge(p_done, count(NC * g + n + 1))
            act.wait_ge(split_done, count(NC * g))
            nc.scalar.activation(qf[:, c, :], bank[BANK_G + c][:, :], ACT.Identity, bias=bqk[:, s:s + 1]).then_inc(p_read, 1)

        def act_high(act, g, c):
            act.wait_ge(p_read, count(NC * (g + 1)))
            if c == 0:
                act.wait_ge(qks_out, count(16 * g))
            nc.scalar.activation(qks[:, 0, c * CH:(c + 1) * CH], qf[:, c, :], ACT.Copy).then_inc(hi_done, 1)

        def act_mid(act, g, c):
            act.wait_ge(rest_done, count(NC * g + c + 1))
            nc.scalar.activation(qks[:, 1, c * CH:(c + 1) * CH], qf[:, c, :], ACT.Copy).then_inc(mid_done, 1)

        def act_hid(act, g, unit):
            n_u = UNITS * g + unit
            act.wait_ge(h_done, count(n_u + 1 + FREE))
            if unit == 0:
                act.wait_ge(dn_done, count(KT * g + FREE))
            nc.scalar.activation(hid[:, 0, unit, :], gated[:, :], ACT.Copy).then_inc(hid_high_done, 1)

        def act_ct(act, g):
            act.wait_ge(ct_done, count(g + 1))
            act.wait_ge(ct_in, count(16 * CPARTS * g))
            nc.scalar.activation(ct[:, :], bank[BANK_X][:, :].bitcast(BF16)[0:CPARTS * GH * NJ, 0:P], ACT.Copy).then_inc(ct_read, 1)

        def acc(c, m):
            t = c * CH // P + 2 * m
            return gacc[:, t:t + 2, :].rearrange("p i e -> p (i e)")

        def act_keep(act, b, n):
            part, k = n // KT, n % KT
            if n == 0:
                act.wait_ge(u_done, count(UNITS * SLOTS * b + FREE))
                act.wait_ge(lt_read, count(4 * (b + 1)))
            nc.scalar.activation(xnF[:, part, k, :], xnT[:, part, k, CH:T].bitcast(F32), ACT.Copy).then_inc(xf_done, 1)

        def act_tanh(act, b, c, m, dst):
            act.wait_ge(dn_read, count(KT * (SLOTS * b + 2 * c + 1) + m + 1))
            nc.scalar.activation(dst, acc(c, m), ACT.Tanh).then_inc(tg_done, 1)

        def act_batch(act, b, last):
            for s in range(SLOTS):
                g = SLOTS * b + s
                for k in range(NSTEP):
                    _, n = step_tokens(k)
                    for h in range(GH):
                        i = GH * k + h
                        act.wait_ge(st_done, count(NPOS * g + i + 1))
                        if h == 0:
                            act.wait_ge(pv_done, count(NSTEP * g + k + 1))
                        nc.scalar.activation(prob[:, k % PR, h, 0:n], bank[BANK_ST + i % 2][:, 0:n], ACT.Exp).then_inc(exp_done, 1)
                        if k % 3 == 1 and h == 1:
                            n_u = UNITS * g + k // 3
                            act.wait_ge(g_done, count(n_u + 1))
                            act.wait_ge(g_read, count(n_u + FREE))
                            if s == 0 and k == 1:
                                act.wait_ge(zg_done, count(4 * b + FREE))
                            if s == 2 and k in (4, 7):
                                act.wait_ge(gate_done, count(4 * b + k // 3 + FREE))
                            t = UNITS * (s % 2) + k // 3
                            nc.scalar.activation(th[:, :], bank[BANK_G][:, :], ACT.Tanh, scale=gsh[:, t:t + 1]).then_inc(th_done, 1)
                        if not (last and s >= SLOTS - 2):
                            if k == 0 and h % 2:
                                act_high(act, g + 2, h // 2)
                            if k in (2, 3) and h == 3:
                                act_mid(act, g + 2, k - 2)
                        if h == 3 and s == 0 and k in KEEP_STEPS:
                            act_keep(act, b, KEEP_STEPS.index(k))
                        if k % 3 == 0 and k and h == 1:
                            act_hid(act, g, k // 3 - 1)
                        if h == 1 and s == 2 and k in (2, 5):
                            act.wait_ge(g_read, count(UNITS * g + k // 3 + 1 + FREE))
                            act_tanh(act, b, 0, k // 3, th[:, :])
                        if s == 1 and not last and k - 1 in LT_STEPS and h == 1:
                            if k - 1 == LT_STEPS[0]:
                                act.wait_ge(p_done, count(NC * SLOTS * (b + 1)))
                                act.wait_ge(v_done, count(4 * (b + 1)))
                                act.wait_ge(xf_done, count(2 * KT * (b + 1)))
                            act_lt(act, b + 1, LT_STEPS.index(k - 1), BANK_X)
                more = not (last and s >= SLOTS - 3)
                act_hid(act, g, UNITS - 1)
                if s == 1 and not last:
                    act.wait_ge(u_done, count(UNITS * (g + 1) + FREE))
                    act_lt(act, b + 1, 2, BANK_X)
                    act_lt(act, b + 1, 3, BANK_G)
                order = CHUNKS_AT[s]
                if more:
                    act_p(act, g + 3, (s + 3) % SLOTS, 0, order[0])
                if not (last and s == SLOTS - 1):
                    act_ct(act, g + 1)
                if more:
                    act_p(act, g + 3, (s + 3) % SLOTS, 1, order[1])
            act.wait_ge(g_read, count(UNITS * SLOTS * (b + 1) + FREE))
            act.wait_ge(hid_low_done, count(UNITS * SLOTS * (b + 1) + FREE))
            for m, dst in enumerate((th, gated)):
                act_tanh(act, b, 1, m, dst[:, :])

        @block.scalar
        def _(act):
            act.wait_ge(w_in, 16 * N_W_IN_ALL)
            nc.scalar.activation(wv[:, 0, :, :].rearrange("p k n -> p (k n)"), wv_full.rearrange("p k n -> p (k n)"), ACT.Copy).then_inc(wv_high, 1)
            for u, x_bank in enumerate(LT_BANKS):
                act_lt(act, 0, u, x_bank)
            act.wait_ge(bias_tp, 1)
            nc.scalar.activation(bqk[:, :], bank[BANK_PV][:, 0:SLOTS], ACT.Copy).then_inc(bias_ev, 1)
            act.wait_ge(bias_ev, 1)
            for c in range(NC):
                act_p(act, 0, 0, c, c)
            for u in range(8):
                act.wait_ge(setup_tp, u + 1)
                w, k, half = (wg, wu)[u // 4], (u % 4) // 2, u % 2
                nc.scalar.activation(w[:, 0, k, half * CH:(half + 1) * CH], bank[u % 4][:, :], ACT.Copy).then_inc(setup_ev, 1)
            for u in range(4):
                tiles = slice(2 * u, 2 * u + 2)
                act.wait_ge(wd_scaled, u + 1)
                nc.scalar.activation(wd[:, 0, tiles, :].rearrange("p i e -> p (i e)"),
                                     wd_full[:, u, :], ACT.Copy).then_inc(wd_high, 1)
            for g in range(1, 3):
                for c in range(NC):
                    act_p(act, g, g, c, c)
            act_ct(act, 0)
            act.wait_ge(credit, 5)
            with act.Fori(0, B - 1) as b:
                act_batch(act, Turn(act, b), False)
            act_batch(act, B - 1, True)

        def pe_lt(pe, b, u, x_bank):
            half, k = LT_UNITS[u]
            for i in range(4):
                t = 4 * half + i
                mm = nc.tensor.transpose(bank[x_bank][:, i * P:(i + 1) * P], xin[:, t, k * P:(k + 1) * P], ident[:, :])
            mm.then_inc(lt_done, 1)

        def pe_p(pe, s, c):
            for k in range(KT):
                for n, (x_part, w_part) in enumerate(SPLIT_TERMS):
                    mm = nc.tensor.matmul(bank[BANK_G + c][:, :], wqk[:, w_part, k, s, :], xnT[:, x_part, k, c * CH:(c + 1) * CH],
                                          start=(k == 0 and n == 0), stop=(k == KT - 1 and n == len(SPLIT_TERMS) - 1))
            mm.then_inc(p_done, 1)

        def pe_v(pe, u, dst):
            for i in range(2):
                t = 2 * u + i
                for k in range(KT):
                    for n, (x_part, w_part) in enumerate(SPLIT_TERMS):
                        mm = nc.tensor.matmul(dst[:, i * E:(i + 1) * E], xnT[:, x_part, k, t * P:(t + 1) * P], wv[:, w_part, k, :],
                                              start=(k == 0 and n == 0), stop=(k == KT - 1 and n == len(SPLIT_TERMS) - 1))
            mm.then_inc(v_done, 1)

        def mx_bank(m, first):
            return bank[m % 4] if first else bank[BANK_MX + m % 2]

        def pe_mx(pe, g, m, par, first=False):
            c, i, h = MX_TILES[m]
            n = min((i + 1) * P - c * CH, CH)
            if not first:
                pe.wait_ge(mx_read, count(NMX * g + m + 1))
            elif m >= 4:
                pe.wait_ge(mx_read, MXR0 + m - 4 + 1)
            nc.tensor.matmul(mx_bank(m, first)[:, 0:n], qs[par][0:KROWS, h, i * P:(i + 1) * P],
                             ks[par][0:KROWS, h, c * CH:c * CH + n], start=True, stop=True).then_inc(mx_done, 1)

        def pe_ct(pe, g):
            pe.wait_ge(cs_done, count(g + 1))
            pe.sem_inc(held_pe, 1)
            nc.tensor.transpose(bank[BANK_X][:, :].bitcast(BF16)[0:CPARTS * GH * NJ, 0:P],
                                cs[:, :, :].rearrange("p a n -> p (a n)"), identb[:, :]).then_inc(ct_done, 1)

        def pe_pv(pe, b, s, k):
            g = SLOTS * b + s
            c, j = STEPS[k]
            first, n = step_tokens(k)
            if k == 0 and s == 0:
                pe.wait_ge(v_read, count(NJ * (b + 1)))
            if j == 0:
                pe.wait_ge(o_read, count(NC * g + c + 1))
            if diagonal(k):
                pe.wait_ge(mask_done, count(8 * g + (k + 1 if c == 0 else k - 3)))
            else:
                pe.wait_ge(exp_done, count(EXP0 + NPOS * g + GH * (k + 1)))
            for h in range(GH):
                at = first - c * CH
                v_at = ((j * PAIRS + s // 2) * GH + h) * VSTEP + D * (s % 2)
                mm = nc.tensor.matmul(bank[BANK_PV][32 * h:32 * h + 32, at:at + n], vals_all[:, v_at:v_at + BLK],
                                      prob[:, k % PR, h, 0:n], start=(j == 0), stop=(at + P == CH and n == P),
                                      tile_position=(0, 32 * h), skip_group_check=True)
            mm.then_inc(pv_done, 1)

        def pe_down(pe, g, s, m):
            pe.wait_ge(hid_low_done, count(UNITS * (g + 1) + FREE))
            for i in range(2):
                tokens = slice((2 * m + i) * P, (2 * m + i + 1) * P)
                for unit in range(UNITS):
                    for n, (h_part, w_part) in enumerate(SPLIT_TERMS):
                        mm = nc.tensor.matmul(bank[BANK_G + m][:, i * E:(i + 1) * E], hid[:, h_part, unit, tokens],
                                              wd[:, w_part, UNITS * (s % 2) + unit, :], start=(unit == 0 and n == 0),
                                              stop=(unit == UNITS - 1 and n == len(SPLIT_TERMS) - 1))
            mm.then_inc(dn_done, 1)

        def pe_gated(pe, b, s, unit, f):
            g = SLOTS * b + s
            t = UNITS * (s % 2) + unit
            half = GATED // 2
            w, dst, done = (wg, bank[BANK_G], g_done) if f < half else (wu, bank[BANK_U], u_done)
            kt, (x_part, w_part) = f % half // len(SPLIT_TERMS), SPLIT_TERMS[f % len(SPLIT_TERMS)]
            if f % half == 0:
                if unit:
                    pe.wait_ge(g_read if f == 0 else h_done, count(UNITS * g + unit + FREE))
                elif s:
                    pe.wait_ge(dn_read, count(KT * g - (1 if f == 0 else 0)))
                else:
                    pe.wait_ge(z_done, count(4 * b + FREE))
            if s == 2 and unit == 0 and f == 0:
                pe.wait_ge(xf_done, count(2 * KT * (b + 1)))
            rows = xnT[:, x_part, kt, 0:CH] if s < 2 else xnF[:, x_part, kt, :]
            mm = nc.tensor.matmul(dst[:, :], w[:, w_part, kt, t * P:(t + 1) * P], rows,
                                  start=(f % half == 0), stop=(f % half == half - 1))
            if f % half == half - 1:
                mm.then_inc(done, 1)

        def pe_batch(pe, b, last):
            for s in range(SLOTS):
                g = SLOTS * b + s
                par = s % 2
                pe.wait_ge(ct_in, count(16 * CPARTS * (g + 1)))
                for k in range(NSTEP):
                    c, j = STEPS[k]
                    first, n = step_tokens(k)
                    if not (last and s == SLOTS - 1):
                        turn = (SLOTS // 2) * b + (s + 1) // 2 + 1
                        if k == 0:
                            pe.wait_ge(q0_in[1 - par], count(16 * TERMS * turn))
                            pe.wait_ge(k0_in[1 - par], count(16 * TERMS * turn))
                        if k == 4:
                            pe.wait_ge(qk1_in[1 - par], count(16 * 2 * TERMS * turn))
                    for h in range(GH):
                        i = GH * k + h
                        pe.wait_ge(exp_done, count(NPOS * g + i + 1))
                        nc.tensor.matmul(bank[BANK_ST + i % 2][:, 0:n], ks[par][:, h, j * P:(j + 1) * P],
                                         qs[par][:, h, first:first + n], start=True, stop=True).then_inc(st_done, 1)
                        if not (last and s == SLOTS - 1):
                            pe_mx(pe, g + 1, i, 1 - par)
                        for n_f in GATED_AT[i]:
                            pe_gated(pe, b, s, n_f // GATED, n_f % GATED)
                    if k:
                        pe_pv(pe, b, s, k - 1)
                    if s == 1 and not last and k in LT_STEPS:
                        u = LT_STEPS.index(k)
                        if u == 0:
                            pe.wait_ge(xn_done, count(NJ * (b + 2)))
                            pe.wait_ge(ct_read, count(g + 1))
                        else:
                            pe.wait_ge(lt_read, count(4 * (b + 1) + u))
                        pe_lt(pe, b + 1, u, BANK_X)
                more = not (last and s >= SLOTS - 3)
                order = CHUNKS_AT[s]
                if s == 1 and not last:
                    pe.wait_ge(lt_read, count(4 * (b + 1) + 2))
                    pe_lt(pe, b + 1, 2, BANK_X)
                    pe.wait_ge(g_read, count(UNITS * (g + 1) + FREE))
                    pe_lt(pe, b + 1, 3, BANK_G)
                if more:
                    if order[0] == 1:
                        pe.wait_ge(h_done, count(UNITS * (g + 1) + FREE))
                    else:
                        pe.wait_ge(g_read, count(UNITS * (g + 1) + FREE))
                    pe_p(pe, (s + 3) % SLOTS, order[0])
                if not (last and s == SLOTS - 1):
                    pe.wait_ge(ct_read, count(g + 1))
                    if s == 0:
                        pe.wait_ge(z_done, count(4 * b + FREE))
                    if s == 1 and not last:
                        pe.wait_ge(lt_read, count(4 * (b + 1) + 3))
                    pe_ct(pe, g + 1)
                pe_pv(pe, b, s, NSTEP - 1)
                pe.wait_ge(h_done, count(UNITS * (g + 1) + FREE))
                if s == 1 and not last:
                    pe.wait_ge(lt_read, count(4 * (b + 2)))
                if more:
                    pe_p(pe, (s + 3) % SLOTS, order[1])
                for m in range(KT):
                    if more:
                        pe.wait_ge(p_read, count(NC * (g + 3) + (m + 1 if order[0] == 0 else NC)))
                    pe_down(pe, g, s, m)
            g = SLOTS * (b + 1) - 1
            if not last:
                for u, x_bank in enumerate((BANK_X, BANK_G, BANK_U, BANK_X)):
                    if u == 0:
                        pe.wait_ge(ct_read, count(g + 2))
                    if u in (1, 2):
                        pe.wait_ge(dn_read, count(KT * (g + 1)))
                    if u == 3:
                        pe.wait_ge(v_read, count(NJ * (b + 1) + 2))
                    pe_v(pe, u, bank[x_bank])
            for u, x_bank in enumerate((BANK_G, BANK_U, BANK_X, BANK_G)):
                if u == 0:
                    pe.wait_ge(dn_read, count(KT * (g + 1)))
                if u < 3 and not last:
                    pe.wait_ge(v_read, count(NJ * (b + 1) + 2 * (u + 2)))
                if u == 2 and last:
                    pe.wait_ge(ct_read, count(g + 1))
                if u == 3:
                    pe.wait_ge(z_done, count(4 * b + 1 + FREE))
                if u % 2 == 0:
                    pe.wait_ge(pair_done, count(PAIR0 + NC * PAIRS * (b + 1) - NC + u // 2 + 1))
                for i in range(2):
                    t = 2 * u + i
                    for k in range(PAIRS):
                        mm = nc.tensor.matmul(bank[x_bank][:, i * E:(i + 1) * E], oT[:, k, t * P:(t + 1) * P], wp[:, k, :],
                                              start=(k == 0), stop=(k == PAIRS - 1))
                mm.then_inc(pj_done, 1)

        @block.tensor
        def _(pe):
            pe.wait_ge(consts, N_CONSTS)
            pe.wait_ge(pool_step, 4)
            pe.wait_ge(xn_done, NJ)
            for u, x_bank in enumerate(LT_BANKS):
                pe_lt(pe, 0, u, x_bank)
            pe.wait_ge(rope_done, 2)
            for s in range(SLOTS):
                mm = nc.tensor.matmul(bank[BANK_PV][:, s:s + 1], bqk_row[0:1, s, :], one[0:1, 0:1], start=True, stop=True)
            mm.then_inc(bias_tp, 1)
            pe.wait_ge(lt_read, 4)
            for c in range(NC):
                pe_p(pe, 0, c)
            for u in range(12):
                if u % 4 == 0:
                    pe.wait_ge(w_conv, count(u // 4 + 1))
                if u >= 4:
                    pe.wait_ge(setup_low, u - 3)
                for i in range(4):
                    if u < 8:
                        src = (gi, ui)[u // 4][:, 4 * (u % 2) + i, ((u % 4) // 2) * P:((u % 4) // 2 + 1) * P]
                    else:
                        t, m = 2 * (u - 8) + i // 2, i % 2
                        src = di[:, m, t * P:(t + 1) * P]
                    mm = nc.tensor.transpose(bank[u % 4][:, i * P:(i + 1) * P], src.bitcast(F32), ident[:, :])
                mm.then_inc(setup_tp, 1)
            for c in range(NC):
                pe.wait_ge(p_read, c + 1)
                pe_p(pe, 1, c)
            pe.wait_ge(wv_low, 1)
            for u, x_bank in enumerate((BANK_X, BANK_G, BANK_U, BANK_X)):
                if u in (1, 2):
                    pe.wait_ge(p_read, NC + u)
                if u == 3:
                    pe.wait_ge(v_read, 2)
                pe_v(pe, u, bank[x_bank])
            for c in range(NC):
                pe.wait_ge(v_read, 2 * (c + 2))
                pe_p(pe, 2, c)
            pe.wait_ge(wd_scaled, 4)
            pe.wait_ge(credit, 5)
            pe.wait_ge(q0_in[0], 16 * TERMS)
            pe.wait_ge(k0_in[0], 16 * TERMS)
            for m in range(4 * GH):
                pe_mx(pe, 0, m, 0, True)
            pe.wait_ge(qk1_in[0], 16 * 2 * TERMS)
            for m in range(4 * GH, NMX):
                pe_mx(pe, 0, m, 0, True)
            pe.wait_ge(setup_low, 8)
            pe.wait_ge(wd_low, 4)
            pe.wait_ge(ones_done, 1)
            pe.wait_ge(mx_read, MXR0 + NMX)
            pe.wait_ge(v_read, NJ)
            pe_ct(pe, 0)
            with pe.Fori(0, B - 1) as b:
                pe_batch(pe, Turn(pe, b), False)
            pe_batch(pe, B - 1, True)

        def dve_stats(dve, b, t):
            if t == 0:
                dve.wait_ge(x_in, count(16 * (b + 1)))
            nc.vector.bn_stats(stats[:, t, :], xin[:, t, :]).then_inc(ln_step, 1)

        def dve_rsqrt(dve, b, step):
            n = LN_STEPS * b + NJ + step
            var, guess, r, tmp = (nv[:, i, :] for i in range(4))
            dve.wait_ge(ln_step, count(n))
            if step == 0:
                dve.sem_inc(held_dve, 1)
                for t in range(NJ):
                    op = nc.vector.bn_aggr(mv[:, t, :], stats[:, t, :])
            elif step == 1:
                op = nc.vector.tensor_scalar(var, mv[:, :, 1], EPS, None, ALU.add)
            elif step == 2:
                op = nc.vector.tensor_scalar(guess.bitcast(I32), var.bitcast(I32), 1, None, ALU.logical_shift_right)
            elif step == 3:
                op = nc.vector.tensor_scalar(r.bitcast(I32), guess.bitcast(I32), -1.0, float(RSQRT_GUESS), ALU.mult, ALU.add)
            elif step % 3 == 1:
                op = nc.vector.tensor_tensor(tmp, r, r, ALU.mult)
            elif step % 3 == 2:
                op = nc.vector.scalar_tensor_tensor(out=tmp, in0=tmp, scalar=-0.5, in1=var, op0=ALU.mult, op1=ALU.mult)
            else:
                op = nc.vector.scalar_tensor_tensor(out=r, in0=tmp, scalar=1.5, in1=r, op0=ALU.add, op1=ALU.mult)
            op.then_inc(ln_step, 1)

        def dve_rows(dve, b, t):
            if t == 0:
                dve.wait_ge(ln_step, count(LN_STEPS * (b + 1)))
            nc.vector.tensor_scalar(xin[:, t, :], xin[:, t, :], mv[:, t, 0:1], nv[:, 2, t:t + 1],
                                    ALU.subtract, ALU.mult).then_inc(xn_done, 1)

        def dve_lt(dve, b, u, x_bank):
            half, k = LT_UNITS[u]
            high, low = (xnT[:, i, k, half * CH:(half + 1) * CH] for i in range(2))
            dve.wait_ge(lt_high, count(4 * b + u + 1))
            nc.vector.tensor_tensor(low, bank[x_bank][:, :], high.bitcast(F32), ALU.subtract).then_inc(lt_read, 1)

        def dve_high(dve, g, c):
            dve.wait_ge(p_read, count(NC * g + c + 1))
            if c == 0:
                dve.wait_ge(qks_out, count(16 * g))
            nc.vector.tensor_copy(qks[:, 0, c * CH:(c + 1) * CH], qf[:, c, :]).then_inc(hi_done, 1)

        def dve_mid(dve, g, c):
            dve.wait_ge(rest_done, count(NC * g + c + 1))
            nc.vector.tensor_copy(qks[:, 1, c * CH:(c + 1) * CH], qf[:, c, :]).then_inc(mid_done, 1)

        def dve_low(dve, g, c):
            dve.wait_ge(mid_done, count(NC * g + c + 1))
            nc.vector.tensor_tensor(qks[:, 2, c * CH:(c + 1) * CH], qf[:, c, :], qks[:, 1, c * CH:(c + 1) * CH],
                                    ALU.subtract).then_inc(split_done, 1)

        def dve_v(dve, b, u, x_bank):
            dve.wait_ge(v_done, count(4 * b + u + 1))
            for i in range(2):
                t = 2 * u + i
                for half in range(2):
                    src, bias = (a.rearrange("p (t s n) -> p t s n", t=PAIRS, s=2)[:, :, half, :].rearrange("p t (q d) -> p t q d", q=GH)
                                 for a in (bank[x_bank][:, i * E:(i + 1) * E], bv[:, :]))
                    op = nc.vector.tensor_tensor(vals[:, t, :, :, (D + 1) * half:(D + 1) * half + D], src, bias, ALU.add)
                op.then_inc(v_read, 1)

        def dve_mx(dve, g, m, first=False):
            c, i, h = MX_TILES[m]
            n = min((i + 1) * P - c * CH, CH)
            src = mx_bank(m, first)[:, 0:n]
            dst = mx[:, h, i:i + 1]
            dve.wait_ge(mx_done, count(NMX * g + m + 1))
            if i * P < (c + 1) * CH:
                if c:
                    dve.wait_ge(mx_read, count(MXR0 + NMX * g + MX_TILES.index((0, i, h)) + 1))
                dve.sem_inc(held_dve, 1)
                nc.vector.tensor_tensor_reduce(src, src, causal[:, CH - n:CH], 1.0, dst if c else LOWEST,
                                               ALU.add, ALU.max, dst).then_inc(mx_read, 1)
            else:
                nc.vector.tensor_reduce(dst, src, AX.X, ALU.max).then_inc(mx_read, 1)

        def dve_cs(dve, g):
            dve.wait_ge(mx_read, count(MXR0 + NMX * (g + 1)))
            dve.wait_ge(ct_done, count(g))
            flat = mx[:, :, :].rearrange("p h i -> p (h i)")
            nc.vector.tensor_scalar(cs[:, 0, :], flat, -1.0, None, ALU.mult).then_inc(cs_step, 1)
            dve.wait_ge(cs_step, count(g + 1))
            nc.vector.scalar_tensor_tensor(out=cs[:, 1, :], in0=flat, scalar=-1.0, in1=cs[:, 0, :],
                                           op0=ALU.mult, op1=ALU.subtract).then_inc(cs_done, 1)

        def dve_turn(dve, g, s, c):
            w = NC * g + c
            dve.wait_ge(pv_done, count(PV0 + NSTEP * g + (4 if c == 0 else NSTEP)))
            dve.wait_ge(on_done, count(w + FREE))
            dve.sem_inc(held_dve, 1)
            nc.vector.transpose(o_rows[:, :, :].rearrange("p n c -> p (n c)"), bank[BANK_PV][:, :]).then_inc(o_read, 1)
            dve.wait_ge(o_read, count(O0 + w + 1))
            nc.vector.reciprocal(rsum[:, :], o_rows[:, :, D * (1 - s % 2)]).then_inc(rsum_done, 1)

        def dve_pair(dve, b, s, c):
            dve.wait_ge(on_done, count(NC * (SLOTS * b + s) + c + 1 + FREE))
            dve.wait_ge(pj_done, count(4 * b + FREE))
            dve.sem_inc(held_dve, 1)
            nc.vector.transpose(oT[:, s // 2, c * CH:(c + 1) * CH], pair[:, c, :, :].rearrange("p n c -> p (n c)")).then_inc(pair_done, 1)

        def dve_gate(dve, b, c, m, src):
            dve.wait_ge(tg_done, count(4 * b + KT * c + m + 1))
            nc.vector.scalar_tensor_tensor(out=acc(c, m), in0=src, scalar=1.0, in1=acc(c, m),
                                           op0=ALU.add, op1=ALU.mult).then_inc(gate_done, 1)

        def dve_batch(dve, b, last):
            for s in range(SLOTS):
                g = SLOTS * b + s
                for k in range(NSTEP):
                    for h in range(GH):
                        i = GH * k + h
                        if not (last and s == SLOTS - 1):
                            dve_mx(dve, g + 1, i)
                        unit = k // 3
                        t = UNITS * (s % 2) + unit
                        if k % 3 == 1 and h == 3:
                            dve.wait_ge(th_done, count(UNITS * g + unit + 1))
                            dve.wait_ge(hid_low_done, count(UNITS * g + unit + FREE))
                            nc.vector.scalar_tensor_tensor(out=gated[:, :], in0=th[:, :], scalar=1.0, in1=bank[BANK_G][:, :],
                                                           op0=ALU.add, op1=ALU.mult).then_inc(g_read, 1)
                        if k % 3 == 2 and h == 2:
                            dve.wait_ge(u_done, count(UNITS * g + unit + 1 + FREE))
                            dve.wait_ge(g_read, count(UNITS * g + unit + 1 + FREE))
                            nc.vector.scalar_tensor_tensor(out=gated[:, :], in0=bank[BANK_U][:, :], scalar=gus[:, t:t + 1],
                                                           in1=gated[:, :], op0=ALU.mult, op1=ALU.mult).then_inc(h_done, 1)
                        if s and (k, h) == (0, 1):
                            dve_turn(dve, g - 1, s - 1, 1)
                        if s == 1 and not last and k - 1 in LT_STEPS and h == 2:
                            dve_lt(dve, b + 1, LT_STEPS.index(k - 1), BANK_X)
                        if s == 2 and (k, h) == (5, 2):
                            dve_pair(dve, b, s - 1, 1)
                        if (k, h) == (5, 1):
                            dve_turn(dve, g, s, 0)
                        if s % 2 and (k, h) == (10, 1):
                            dve_pair(dve, b, s, 0)
                        if s == 2 and k in (3, 6) and h == 0:
                            dve_gate(dve, b, 0, k // 3 - 1, th[:, :])
                        if s == 0 and not last and i in STATS_AT:
                            dve_stats(dve, b + 1, STATS_AT.index(i))
                        if s == 0 and not last and i >= NPOS - RSQRT_STEPS:
                            dve_rsqrt(dve, b + 1, i - NPOS + RSQRT_STEPS)
                if not (last and s == SLOTS - 1):
                    dve_cs(dve, g + 1)
                if s == 1 and not last:
                    dve_lt(dve, b + 1, 2, BANK_X)
                    dve_lt(dve, b + 1, 3, BANK_G)
                for m in range(KT):
                    dve.wait_ge(dn_done, count(KT * g + m + 1 + FREE))
                    if s % 2 == 0:
                        dve.wait_ge(y_done, count(4 * b + FREE))
                        nc.vector.tensor_copy(acc(s // 2, m), bank[BANK_G + m][:, :]).then_inc(dn_read, 1)
                    else:
                        dve.wait_ge(dn_read, count(KT * g))
                        nc.vector.tensor_tensor(acc(s // 2, m), bank[BANK_G + m][:, :], acc(s // 2, m), ALU.add).then_inc(dn_read, 1)
            dve_turn(dve, SLOTS * (b + 1) - 1, SLOTS - 1, 1)
            for m, src in enumerate((th, gated)):
                dve_gate(dve, b, 1, m, src[:, :])
            dve_pair(dve, b, SLOTS - 1, 1)
            if not last:
                dve.wait_ge(pv_done, count(PV0 + NSTEP * SLOTS * (b + 1)))
                for u, x_bank in enumerate((BANK_X, BANK_G, BANK_U, BANK_X)):
                    dve_v(dve, b + 1, u, x_bank)
            for u, x_bank in enumerate((BANK_G, BANK_U, BANK_X, BANK_G)):
                s_rows = z[u % 2][:, :]
                dve.wait_ge(pj_done, count(4 * b + u + 1 + FREE))
                dve.wait_ge(gate_done, count(4 * (b + 1) + FREE))
                if u >= 2:
                    dve.wait_ge(zg_done, count(4 * b + u - 1 + FREE))
                nc.vector.tensor_tensor(s_rows.rearrange("p (i e) -> p i e", i=2), bank[x_bank][:, :].rearrange("p (i e) -> p i e", i=2),
                                        bp[:, :].rearrange("p (o e) -> p o e", o=1).broadcast_to([P, 2, E]), ALU.add).then_inc(z_done, 1)
                dve.wait_ge(z_done, count(4 * b + u + 1 + FREE))
                nc.vector.tensor_tensor(acc(u // 2, u % 2), s_rows, acc(u // 2, u % 2), ALU.mult).then_inc(zg_done, 1)

        @block.vector
        def _(dve):
            nc.vector.memset(nothing[:, 13:14], 0.0).then_inc(exp_done, EXP0)
            nc.vector.memset(nothing[:, 14:15], 0.0).then_inc(mx_read, MXR0)
            nc.vector.memset(nothing[:, 15:16], 0.0).then_inc(pv_done, PV0)
            nc.vector.memset(nothing[:, 16:17], 0.0).then_inc(o_read, O0)
            nc.vector.memset(nothing[:, 17:18], 0.0).then_inc(pair_done, PAIR0)
            for i, done in enumerate((pj_done, z_done, gate_done, dn_done, h_done, hid_low_done, zg_done, y_done, on_done, g_read, u_done, out_done)):
                nc.vector.memset(nothing[:, i:i + 1], 0.0).then_inc(done, FREE)
            nc.vector.memset(nothing[:, 18:19], 0.0).then_inc(credit, 5)
            for t in range(NJ):
                dve_stats(dve, 0, t)
            for step in range(RSQRT_STEPS):
                dve_rsqrt(dve, 0, step)
            for t in range(NJ):
                dve_rows(dve, 0, t)
            dve.wait_ge(w_in, 16 * N_W_IN_ALL)
            n = 0
            for r, (src, rows) in enumerate(ROPE_SOURCES):
                direct, cross = rtmp[r][0:rows, :], rtmp2[r][0:rows, :]
                dve.wait_ge(rope_products, 3 * (r + 1))
                if r == KT:
                    for side in range(2):
                        op = nc.vector.tensor_tensor(bqk_row[:, :, side * 64:(side + 1) * 64],
                                                     *(a[:, side * E:(side + 1) * E].rearrange("p (s n) -> p s n", s=SLOTS) for a in (direct, cross)), ALU.add)
                    op.then_inc(rope_done, 1)
                    continue
                nc.vector.tensor_tensor(direct, direct, cross, ALU.add).then_inc(rope_step, 1)
                n += 1
                for part in range(2):
                    dve.wait_ge(rope_step, n)
                    for side in range(2):
                        full = direct[:, side * E:(side + 1) * E].rearrange("p (s n) -> p s n", s=SLOTS)
                        high, low = (wqk[:, i, r, :, side * 64:(side + 1) * 64] for i in range(2))
                        if part == 0:
                            nc.vector.tensor_copy(high, full).then_inc(rope_step, 1)
                            n += 1
                        else:
                            op = nc.vector.tensor_tensor(low, full, high.bitcast(F32), ALU.subtract)
                if r:
                    op.then_inc(rope_done, 1)
            for u, x_bank in enumerate(LT_BANKS):
                dve_lt(dve, 0, u, x_bank)
            nc.vector.tensor_scalar(gsh[:, :], gsc[:, :], 0.5, None, ALU.mult).then_inc(rope_step, 1)
            dve.wait_ge(rope_step, n + 1)
            nc.vector.tensor_tensor(gus[:, :], gsh[:, :], usc[:, :], ALU.mult).then_inc(rope_step, 1)
            dve.wait_ge(quant_in, 16 * 2)
            for w in (gi, ui):
                nc.vector.tensor_scalar(w.bitcast(F32), w, -ZERO_POINT, None, ALU.add).then_inc(w_conv, 1)
            for part in (dve_high, dve_mid, dve_low):
                for c in range(NC):
                    part(dve, 0, c)
            dve.wait_ge(down_in, 16)
            nc.vector.tensor_scalar(di.bitcast(F32), di, -ZERO_POINT, None, ALU.add).then_inc(w_conv, 1)
            for u in range(8):
                w, k, half = (wg, wu)[u // 4], (u % 4) // 2, u % 2
                cols = slice(half * CH, (half + 1) * CH)
                dve.wait_ge(setup_ev, u + 1)
                nc.vector.tensor_tensor(w[:, 1, k, cols], bank[u % 4][:, :], w[:, 0, k, cols].bitcast(F32), ALU.subtract).then_inc(setup_low, 1)
            for u in range(4):
                dve.wait_ge(setup_tp, 8 + u + 1)
                nc.vector.scalar_tensor_tensor(out=wd_full[:, u, :].rearrange("p (i e) -> p i e", i=2), in0=bank[u][:, :].rearrange("p (i e) -> p i e", i=2),
                                               scalar=0.5, in1=dsc.rearrange("p (o e) -> p o e", o=1).broadcast_to([P, 2, E]),
                                               op0=ALU.mult, op1=ALU.mult).then_inc(wd_scaled, 1)
            for part in (dve_high, dve_mid, dve_low):
                for c in range(NC):
                    part(dve, 1, c)
            dve.wait_ge(ones_done, 1)
            for u, x_bank in enumerate((BANK_X, BANK_G, BANK_U, BANK_X)):
                dve_v(dve, 0, u, x_bank)
            for m in range(NMX):
                dve_mx(dve, 0, m, True)
            dve_cs(dve, 0)
            with dve.Fori(0, B - 1) as b:
                dve_batch(dve, Turn(dve, b), False)
            dve_batch(dve, B - 1, True)


N_W_IN_ALL = 2 + 2 * GH + 4

_INS = ['L0_attn_x', 'L0_attn_w_attn', 'L0_attn_b_attn', 'L0_attn_w_proj', 'L0_attn_b_proj', 'L0_ffn_gate_w',
        'L0_ffn_gate_scale', 'L0_ffn_up_w', 'L0_ffn_up_scale', 'L0_ffn_down_w', 'L0_ffn_down_scale']


def _rope_rows():
    import numpy as np

    freqs = np.float32(10000.0) ** (-(np.arange(0, D, 2, dtype=np.float32) / np.float32(D)))
    angle = np.outer(np.arange(H, dtype=np.float32), freqs.astype(np.float32)).astype(np.float32)
    cos, sin = np.cos(angle).astype(np.float32), np.sin(angle).astype(np.float32)
    cos = np.stack([cos, cos], -1).reshape(1, E)
    sin = np.stack([-sin, sin], -1).reshape(1, E)
    return np.concatenate([cos, cos], 1), np.concatenate([sin, sin], 1)


def kernel(**inputs):
    import numpy as _np
    import concourse.bacc as _bacc
    from concourse import mybir as _mybir
    from concourse.bass_utils import run_bass_kernel_spmd as _run

    nc = _bacc.Bacc("TRN2", target_bir_lowering=False, num_devices=1)
    arrays, args = {}, []
    rope_cos, rope_sin = _rope_rows()
    named = [(name, inputs[name]) for name in _INS] + [("rope_cos", rope_cos), ("rope_sin", rope_sin)]
    for name, a in named:
        a = _np.ascontiguousarray(a)
        arrays[f"in_{name}"] = a
        args.append(nc.dram_tensor(f"in_{name}", a.shape, _mybir.dt.from_np(a.dtype), kind="ExternalInput").ap())
    args.append(nc.dram_tensor("out_y", (B, T, E), F32, kind="ExternalOutput").ap())
    build(nc, *args)
    r = _run(nc, [arrays], core_ids=[0])
    return r.results[0]["out_y"]
```
